# Optimizing a Trainium2 kernel written in Bass

```python
import numpy as np
import jax
import jax.numpy as jnp

def _softmax(x, axis=-1):
    return jax.nn.softmax(x, axis=axis)

def _gelu(x):
    return jax.nn.gelu(x, approximate=True)

def _silu(x):
    return jax.nn.silu(x)

def _sigmoid(x):
    return jax.nn.sigmoid(x)

def _layernorm(x, axis=-1, eps=1e-05):
    m = jnp.mean(x, axis=axis, keepdims=True)
    v = jnp.var(x, axis=axis, keepdims=True)
    return (x - m) / jnp.sqrt(v + eps)

def _scatter_add(tgt, idx, src, axis=0):
    return tgt.at[idx].add(src)

def _segment_sum(src, seg, n):
    return jax.ops.segment_sum(src, seg, n)
kernel_name = 'mk_sandwich_d1_jaxref_r8_70da3d'

def setup_inputs(seed: int=0):
    np.random.seed(seed)
    _w = jnp.asarray

    def _L0_attn_setup():
        import jax, jax.numpy as jnp
        import numpy as np
        DIM = 256
        HEAD_DIM = 64
        D_H = 64
        ATTN_HEAD_DIM = 128
        NH = DIM // HEAD_DIM
        NAH = DIM // ATTN_HEAD_DIM
        BATCH, SEQ = (1, 512)
        CHUNK = 128
        WINDOW = 128
        BASE_LR = 0.01
        BASE_LR_INV = float(BASE_LR + np.log(-np.expm1(-BASE_LR)))
        NS_COEFFS = [(4.0848, -6.8946, 2.927), (3.9505, -6.3029, 2.6377), (3.7418, -5.5913, 2.3037), (2.8769, -3.1427, 1.2046), (2.8366, -3.0525, 1.2012)]

        def _silu_bp(dy, x):
            s = jax.nn.sigmoid(x)
            return dy * s * (1 + x * (1 - s))

        def _l2norm(t):
            return t / (jnp.linalg.norm(t, axis=-1, keepdims=True) + 1e-05)

        def _newtonschulz5(G):
            X = G
            tr = G.shape[1] > G.shape[2]
            if tr:
                X = X.transpose(0, 2, 1)
            X = X / (jnp.sqrt(jnp.sum(X * X, axis=(1, 2), keepdims=True)) + 1e-07)
            for a, b, c in NS_COEFFS:
                A = X @ X.transpose(0, 2, 1)
                B = b * A + c * (A @ A)
                X = a * X + B @ X
            if tr:
                X = X.transpose(0, 2, 1)
            return X
        key = jax.random.key(seed)
        ks = jax.random.split(key, 12)
        f32 = jnp.float32
        return {'x': jax.random.normal(ks[0], (BATCH, SEQ, DIM), f32), 'Wqkv': jax.random.normal(ks[1], (DIM, 3 * DIM), f32) / np.sqrt(DIM), 'Wlr': jax.random.normal(ks[2], (DIM, 3 * NH), f32) / np.sqrt(DIM), 'Wm': jax.random.normal(ks[3], (DIM, NH), f32) / np.sqrt(DIM), 'bm': jnp.zeros((NH,), f32), 'Ws': jax.random.normal(ks[4], (DIM, NH), f32) / np.sqrt(DIM), 'bs': jnp.zeros((NH,), f32), 'Wo': jax.random.normal(ks[5], (DIM, DIM), f32) / np.sqrt(DIM), 'w0': jax.random.normal(ks[6], (NH, D_H, HEAD_DIM), f32) / np.sqrt(HEAD_DIM), 'w1': jax.random.normal(ks[7], (NH, HEAD_DIM, D_H), f32) / np.sqrt(D_H), 'w2': jax.random.normal(ks[8], (NH, D_H, HEAD_DIM), f32) / np.sqrt(HEAD_DIM), 'o_norm_g': jnp.ones((HEAD_DIM,), f32), 'qk_scale': jnp.ones((DIM, 2), f32), 'qk_offset': jnp.zeros((DIM, 2), f32)}
    _L0_attn_in = _L0_attn_setup()

    def _L0_ffn_setup():
        import jax, jax.numpy as jnp
        import numpy as np
        L, N, E, H, K = (256, 8, 256, 1024, 8)
        key = jax.random.key(seed)
        ks = jax.random.split(key, 6)
        return {'x': jax.random.normal(ks[0], (L, N, E), dtype=jnp.float32), 'proj1': jax.random.normal(ks[1], (H, E), dtype=jnp.float32) * 0.02, 'proj1_bias': jax.random.normal(ks[2], (H,), dtype=jnp.float32) * 0.02, 'proj2': jax.random.normal(ks[3], (E, H), dtype=jnp.float32) * 0.02, 'proj2_bias': jax.random.normal(ks[4], (E,), dtype=jnp.float32) * 0.02, 'gate_w': jax.random.normal(ks[5], (E, K), dtype=jnp.float32)}
    _L0_ffn_in = _L0_ffn_setup()
    _d = {'L0_attn_x': _L0_attn_in['x'], 'L0_attn_Wqkv': _L0_attn_in['Wqkv'], 'L0_attn_Wlr': _L0_attn_in['Wlr'], 'L0_attn_Wm': _L0_attn_in['Wm'], 'L0_attn_bm': _L0_attn_in['bm'], 'L0_attn_Ws': _L0_attn_in['Ws'], 'L0_attn_bs': _L0_attn_in['bs'], 'L0_attn_Wo': _L0_attn_in['Wo'], 'L0_attn_w0': _L0_attn_in['w0'], 'L0_attn_w1': _L0_attn_in['w1'], 'L0_attn_w2': _L0_attn_in['w2'], 'L0_attn_o_norm_g': _L0_attn_in['o_norm_g'], 'L0_attn_qk_scale': _L0_attn_in['qk_scale'], 'L0_attn_qk_offset': _L0_attn_in['qk_offset'], 'L0_ffn_proj1': _L0_ffn_in['proj1'], 'L0_ffn_proj1_bias': _L0_ffn_in['proj1_bias'], 'L0_ffn_proj2': _L0_ffn_in['proj2'], 'L0_ffn_proj2_bias': _L0_ffn_in['proj2_bias'], 'L0_ffn_gate_w': _L0_ffn_in['gate_w']}
    _x0 = _d['L0_attn_x']
    _d['L0_attn_x'] = jax.random.normal(jax.random.fold_in(jax.random.key(seed), 1), (4, 512, 256), dtype=_x0.dtype)
    del _x0
    return _d

def reference(L0_attn_x, L0_attn_Wqkv, L0_attn_Wlr, L0_attn_Wm, L0_attn_bm, L0_attn_Ws, L0_attn_bs, L0_attn_Wo, L0_attn_w0, L0_attn_w1, L0_attn_w2, L0_attn_o_norm_g, L0_attn_qk_scale, L0_attn_qk_offset, L0_ffn_proj1, L0_ffn_proj1_bias, L0_ffn_proj2, L0_ffn_proj2_bias, L0_ffn_gate_w):

    def _L0_attn_ref(x, Wqkv, Wlr, Wm, bm, Ws, bs, Wo, w0, w1, w2, o_norm_g, qk_scale, qk_offset):
        import jax, jax.numpy as jnp
        import numpy as np
        DIM = 256
        HEAD_DIM = 64
        D_H = 64
        ATTN_HEAD_DIM = 128
        NH = DIM // HEAD_DIM
        NAH = DIM // ATTN_HEAD_DIM
        BATCH, SEQ = (1, 512)
        CHUNK = 128
        WINDOW = 128
        BASE_LR = 0.01
        BASE_LR_INV = float(BASE_LR + np.log(-np.expm1(-BASE_LR)))
        NS_COEFFS = [(4.0848, -6.8946, 2.927), (3.9505, -6.3029, 2.6377), (3.7418, -5.5913, 2.3037), (2.8769, -3.1427, 1.2046), (2.8366, -3.0525, 1.2012)]

        def _silu_bp(dy, x):
            s = jax.nn.sigmoid(x)
            return dy * s * (1 + x * (1 - s))

        def _l2norm(t):
            return t / (jnp.linalg.norm(t, axis=-1, keepdims=True) + 1e-05)

        def _newtonschulz5(G):
            X = G
            tr = G.shape[1] > G.shape[2]
            if tr:
                X = X.transpose(0, 2, 1)
            X = X / (jnp.sqrt(jnp.sum(X * X, axis=(1, 2), keepdims=True)) + 1e-07)
            for a, b, c in NS_COEFFS:
                A = X @ X.transpose(0, 2, 1)
                B = b * A + c * (A @ A)
                X = a * X + B @ X
            if tr:
                X = X.transpose(0, 2, 1)
            return X
        b, L, d = x.shape
        attn_qkv = x @ Wqkv
        ttt = jax.nn.silu(attn_qkv).reshape(b, L, 3, NH, HEAD_DIM)

        def heads(t):
            return t.transpose(0, 2, 1, 3).reshape(b * NH, L, HEAD_DIM)
        q = _l2norm(heads(ttt[:, :, 0]))
        k = _l2norm(heads(ttt[:, :, 1]))
        v = heads(ttt[:, :, 2])
        lr = jax.nn.softplus(x @ Wlr + BASE_LR_INV).reshape(b, L, NH, 3, 1)

        def lr_h(i):
            return lr[:, :, :, i, :].transpose(0, 2, 1, 3).reshape(b * NH, L, 1)
        lr0, lr1, lr2 = (lr_h(0), lr_h(1), lr_h(2))
        mom = jax.nn.sigmoid(x @ Wm + bm).reshape(b, L, NH, 1)
        mom = mom.transpose(0, 2, 1, 3).reshape(b * NH, L, 1)
        w0b = jnp.tile(w0, (b, 1, 1))
        w1b = jnp.tile(w1, (b, 1, 1))
        w2b = jnp.tile(w2, (b, 1, 1))
        n0 = jnp.linalg.norm(w0b, axis=2, keepdims=True)
        n1 = jnp.linalg.norm(w1b, axis=2, keepdims=True)
        n2 = jnp.linalg.norm(w2b, axis=2, keepdims=True)
        nc = L // CHUNK

        def chunkit(t):
            return t.reshape(b * NH, nc, CHUNK, -1).transpose(1, 0, 2, 3)
        xs = tuple(map(chunkit, (q, k, v, lr0, lr1, lr2, mom)))

        def step(carry, xi):
            W0, W1, W2, M0, M1, M2 = carry
            qi, ki, vi, l0, l1, l2, mi = xi
            hid = jnp.einsum('bcd,bhd->bch', qi, W2)
            gate = jax.nn.silu(jnp.einsum('bcd,bhd->bch', qi, W0))
            out = jnp.einsum('bch,boh->bco', gate * hid, W1)
            gba = jnp.einsum('bcd,bhd->bch', ki, W0)
            hbm = jnp.einsum('bcd,bhd->bch', ki, W2)
            sg = jax.nn.silu(gba)
            hidden = sg * hbm
            dhidden = jnp.einsum('bco,boh->bch', vi, W1)
            dhbm = dhidden * sg
            dgba = _silu_bp(dhidden * hbm, gba)
            dw1 = jnp.einsum('bco,bch->boh', vi, hidden * l1)
            dw0 = jnp.einsum('bch,bcd->bhd', dgba, ki * l0)
            dw2 = jnp.einsum('bch,bcd->bhd', dhbm, ki * l2)
            mm = jnp.mean(mi, axis=1, keepdims=True)
            dw0 = dw0 + M0 * mm
            dw1 = dw1 + M1 * mm
            dw2 = dw2 + M2 * mm
            M0n, M1n, M2n = (dw0, dw1, dw2)
            dw0 = _newtonschulz5(dw0)
            dw1 = _newtonschulz5(dw1)
            dw2 = _newtonschulz5(dw2)

            def renorm(Wn, n):
                return Wn / (jnp.linalg.norm(Wn, axis=2, keepdims=True) + 1e-05) * n
            return ((renorm(W0 + dw0, n0), renorm(W1 + dw1, n1), renorm(W2 + dw2, n2), M0n, M1n, M2n), out)
        init = (w0b, w1b, w2b, jnp.zeros_like(w0b), jnp.zeros_like(w1b), jnp.zeros_like(w2b))
        _, outs = jax.lax.scan(step, init, xs)
        ttt_out = outs.transpose(1, 0, 2, 3).reshape(b * NH, L, HEAD_DIM)
        ms = jnp.mean(ttt_out * ttt_out, axis=-1, keepdims=True)
        ttt_out = ttt_out * jax.lax.rsqrt(ms + 1e-05) * o_norm_g
        scale = jax.nn.silu(x @ Ws + bs).reshape(b, L, NH, 1)
        scale = scale.transpose(0, 2, 1, 3).reshape(b * NH, L, 1)
        ttt_out = (ttt_out * scale).reshape(b, NH, L, HEAD_DIM)
        ttt_out = ttt_out.transpose(0, 2, 1, 3).reshape(b, L, d)
        aq, ak, av = jnp.split(attn_qkv, 3, axis=-1)
        aq = aq * qk_scale[:, 0] + qk_offset[:, 0]
        ak = ak * qk_scale[:, 1] + qk_offset[:, 1]
        aq = aq.reshape(b, L, NAH, ATTN_HEAD_DIM)
        ak = ak.reshape(b, L, NAH, ATTN_HEAD_DIM)
        av = av.reshape(b, L, NAH, ATTN_HEAD_DIM)
        W_ = WINDOW
        nb = L // W_
        kpad = jnp.pad(ak, ((0, 0), (W_, 0), (0, 0), (0, 0)))
        vpad = jnp.pad(av, ((0, 0), (W_, 0), (0, 0), (0, 0)))
        widx = jnp.arange(nb)[:, None] * W_ + jnp.arange(2 * W_)[None, :]
        kwin = kpad[:, widx]
        vwin = vpad[:, widx]
        qblk = aq.reshape(b, nb, W_, NAH, ATTN_HEAD_DIM)
        scores = jnp.einsum('bnqhd,bnkhd->bnhqk', qblk, kwin) / np.sqrt(ATTN_HEAD_DIM)
        qi_ = jnp.arange(W_)[:, None]
        kj = jnp.arange(2 * W_)[None, :]
        base = (kj >= qi_) & (kj <= qi_ + W_)
        kvalid = jnp.arange(nb)[:, None] * W_ - W_ + jnp.arange(2 * W_)[None, :] >= 0
        mask = base[None, :, :] & kvalid[:, None, :]
        scores = jnp.where(mask[None, :, None], scores, -jnp.inf)
        probs = jax.nn.softmax(scores, axis=-1)
        attn_out = jnp.einsum('bnhqk,bnkhd->bnqhd', probs, vwin).reshape(b, L, d)
        return (ttt_out + attn_out) @ Wo

    def _L0_ffn_ref(x, proj1, proj1_bias, proj2, proj2_bias, gate_w):
        import jax, jax.numpy as jnp
        import numpy as np
        L, N, E, H, K = (256, 8, 256, 1024, 8)
        dst = jnp.argmax(jnp.einsum('lne,ek->lnk', x, gate_w), axis=-1)
        h = jax.nn.gelu(jnp.einsum('lne,he->lnh', x, proj1) + proj1_bias, approximate=False)
        out = jnp.einsum('lnh,eh->lne', h, proj2) + proj2_bias
        del dst
        return out
    x = L0_attn_x
    x = x + _layernorm(_L0_attn_ref(_layernorm(x, axis=-1), L0_attn_Wqkv, L0_attn_Wlr, L0_attn_Wm, L0_attn_bm, L0_attn_Ws, L0_attn_bs, L0_attn_Wo, L0_attn_w0, L0_attn_w1, L0_attn_w2, L0_attn_o_norm_g, L0_attn_qk_scale, L0_attn_qk_offset), axis=-1)
    x = x + _layernorm(_L0_ffn_ref(_layernorm(x, axis=-1), L0_ffn_proj1, L0_ffn_proj1_bias, L0_ffn_proj2, L0_ffn_proj2_bias, L0_ffn_gate_w), axis=-1)
    return x

_drawn_inputs = setup_inputs


def setup_inputs(seed=0):
    import zlib

    import numpy as np

    out = dict(_drawn_inputs(seed))
    spreads = {'L0_attn_bm': (0.0, 0.1),
     'L0_attn_bs': (0.0, 0.1),
     'L0_attn_o_norm_g': (1.0, 0.2),
     'L0_attn_qk_scale': (1.0, 0.2),
     'L0_attn_qk_offset': (0.0, 0.1)}
    factors = {}
    for name, (base, spread) in spreads.items():
        noise = np.random.default_rng([zlib.crc32(name.encode()), seed]).standard_normal(out[name].shape)
        drawn = base * np.exp(spread * noise) if base else spread * noise
        out[name] = jnp.asarray(drawn.astype(out[name].dtype))
    for name, factor in factors.items():
        out[name] = (out[name] * factor).astype(out[name].dtype)
    return out
```

```python
from contextlib import ExitStack

import numpy as np

import concourse.bass as bass
from concourse import mybir

F32 = mybir.dt.float32
ALU = mybir.AluOpType
ACT = mybir.ActivationFunctionType
AX = mybir.AxisListType

P = 128
BATCH, SEQ, DIM = 4, 512, 256
CHUNK = 128
CHUNKS = SEQ // CHUNK
HD = 64
NH = DIM // HD
KC = DIM // P
HID = 1024
HC = HID // P
NAH = 2
SMALL = 5 * NH
LN_EPS = 1e-5
BASE_LR = 0.01
BASE_LR_INV = float(BASE_LR + np.log(-np.expm1(-BASE_LR)))
SCALE = float(P) ** -0.5
NEG = -1.0e30
NS = [(4.0848, -6.8946, 2.927), (3.9505, -6.3029, 2.6377), (3.7418, -5.5913, 2.3037),
      (2.8769, -3.1427, 1.2046), (2.8366, -3.0525, 1.2012)]
NIT = len(NS)
GRAD_GAIN = 4.0

NS_F, NS_E, NS_S = [], [], 1.0
for _a, _b, _c in NS:
    NS_F.append(_c * NS_S * NS_S / _b)
    NS_E.append(_b * NS_S * NS_S / _a)
    NS_S *= _a

G_W1, G_W2, G_W0 = 0, 1, 2


class Signal:

    def __init__(self, sem, per_chunk):
        self.sem, self.per_chunk = sem, per_chunk

    def __call__(self, c, n):
        return self.sem, c * self.per_chunk + n


RISES = dict(
    ln1_stats=1, ln1_mv=1, ln1_var=1, ln1_rstd=1, xn=1, xT_ps=2, xnT=2, small_ps=1, small=1,
    lr_neg=1, lr_exp=1, lr_log=1, lr=1, ms_tanh=1, ms=1, mm_ps=1, mm=1, decayed=3,
    qk_ps=4, qk_raw=4, v_ps=4, v_raw=4, sig=4, silu=4, sq=4, ssq=4, nq=4, nq_eps=4, rq=4, qn=4, klv=4,
    tr_ps=10, att_T=4, ttt_T=6,
    gba_ps=2, gba_tanh=2, dh_ps=1, dh=1, sg=2, el=2, one_t=2, dhbm=2, dsig=2, dgba=2, dw_ps=3,
    fw_ps=2, fw_tanh=2, fw_silu=2, gT=2, out_ps=2, out_sq=1, out_ms=1, out_var=1, out_rs=1, out_f=1, y=1, yg=1,
    mom=3, mom_sq=3, mom_ss=3, ss_ps=3, ss=3, fro=3, fro_eps=3, rfro=3, x0=3,
    xt_ps=15, XT=15, a_ps=15, A=15, b_ps=15, B=15, x_ps=15, X=15, V=3,
    u_sq=3, u_ss=3, u_n=3, u_eps=3, u_r=3, u_f=3, W=3, w_ps=3, WT=3,
    s_ps=4, masked=4, neg_max=4, prob=4, psum_r=4, pt_ps=4, pT=4, pv_ps=4, comb=4, ct_ps=4, cT=4,
    k_prev=1, v_prev=1, m_prev=1,
    wo_ps=4, wo_st=4, wo_mv=4, wo_var=4, wo_rstd=4, wo_n=4, x1=4,
    l2_st=4, l2_mv=4, l2_var=4, l2_rstd=4, xn2=4, nt_ps=4, xn2T=4, f1_ps=8, h=8,
    f2_ps=4, f2=4, f2_st=4, f2_mv=4, f2_var=4, f2_rstd=4, f2_n=4, outb=4, x_res=1,
    x_in=16, stored=64,
)

PROJ_A = [("LN1",), ("XT",), ("SM",)]
QKV = [("QK", b) for b in range(4)]


def update_slots():
    chain = [(kind, it) for it in range(NIT) for kind in ("TX", "NA", "NB", "NX")]
    macros = []
    for m in range(len(chain) + 4):
        slots = []
        for g in range(3):
            k = m - g
            if 0 <= k < len(chain):
                slots.append((chain[k][0], chain[k][1], g))
                if chain[k] == ("NX", NIT - 2):
                    slots.append(("NV", g))
            if k == len(chain):
                slots.append(("RN", g))
            if k == len(chain) + 1:
                slots.append(("WX", g))
        macros.append(slots)
    return macros


def merge(macros, filler):
    cost = {"S": .9, "PT": .3, "PV": .9, "CT": .15, "WO": .9, "NT": .15, "F1": 1.75, "F2": 3.5, "QK": 1.75,
            "VV": .9, "TR": .3, "XT": .6, "SM": .4}
    total = sum(cost.get(s[0], 0) for s in filler)
    out, k, done = [], 0, 0.0
    n = sum(len(m) for m in macros)
    at = 0
    for m in macros:
        for s in m:
            out.append(s)
            at += 1
            while k < len(filler) and done <= total * at / n:
                out.append(filler[k])
                done += cost.get(filler[k][0], 0)
                k += 1
    return out + filler[k:]


ATT = [("S", 0), ("S", 1), ("PT", 0), ("S", 2), ("PV", 0), ("PT", 1), ("S", 3), ("PV", 1), ("CT", 0), ("PT", 2)]
ATT_END = [("PV", 2), ("PT", 3), ("CT", 1), ("WO", 0), ("PV", 3), ("CT", 2), ("WON", 0), ("WO", 1), ("CT", 3),
           ("L2", 0), ("WON", 1), ("WO", 2), ("L2N", 0), ("L2", 1), ("WON", 2), ("WO", 3), ("NT", 0), ("L2N", 1), ("L2", 2),
           ("WON", 3), ("NT", 1), ("L2N", 2), ("L2", 3), ("PRV",)]
MLP_IN = [("NT", 2), ("L2N", 3), ("NT", 3), ("XRES",)] + [("F1", n) for n in range(HC)]
MLP_OUT = [("F2", 0), ("F2", 1), ("F2N", 0), ("F2", 2), ("F2N", 1), ("F2", 3), ("F2N", 2), ("F2N", 3)]


def proj(b):
    return [("QK", b), ("VV", b), ("SI", b), ("NQ", b)]


RAW_T = [("TR", u) for u in range(4)]
TTT_T = [("TR", u) for u in range(4, 10)]

FORWARD = [("FW", 0), ("FE", 0), ("FW", 1), ("FE", 1), ("OUT", 0), ("OUT", 1), ("OE",)]
BODY = [("GB", 0), ("DH",), ("GB", 1), ("FW", 0), ("LN1",), ("EL", 0), ("FE", 0), ("XT",), ("ELB", 0), ("FW", 1), ("SM",),
        ("DW", 0), ("EL", 1), ("FE", 1), ("OUT", 0), ("ELB", 1), ("S", 0), ("OUT", 1), ("DW", 1), ("S", 1), ("MU", 0),
        ("OE",), ("SS", 0), ("MU", 1), ("PT", 0), ("SN", 0), ("SS", 1), ("MU", 2), ("OY",), ("S", 2), ("SN", 1), ("SS", 2), ("PT", 1), ("SN", 2)]
BODY += merge(update_slots(), [("S", 3), ("PV", 0), ("PT", 2), ("SP",), ("PV", 1), ("CT", 0), ("MS",)] + ATT_END + [("MM",)]
              + proj(0) + [("NT", 2), ("L2N", 3)] + proj(1) + [("NT", 3), ("XRES",)] + [("F1", 0), ("F1", 1), ("F1", 2)]
              + proj(2) + [("F1", 3), ("F1", 4), ("F1", 5)] + proj(3) + [("F1", 6), ("F1", 7)] + RAW_T[:2] + [("F2", 0)]
              + RAW_T[2:] + [("F2", 1)] + TTT_T[:3] + [("F2N", 0), ("F2", 2), ("F2N", 1)] + TTT_T[3:] + [("MP",), ("F2", 3), ("F2N", 2), ("F2N", 3)])
FIRST = [("LN1",), ("XT",), ("SM",), ("SP",), ("MS",), ("MM",)] + proj(0) + proj(1) + proj(2) + proj(3) + RAW_T + TTT_T + [("MP",)]
LAST = [("FW", 0), ("FE", 0), ("FW", 1), ("S", 0), ("FE", 1), ("S", 1), ("OUT", 0), ("OUT", 1), ("OE",), ("PT", 0), ("OY",),
        ("S", 2), ("PV", 0), ("PT", 1), ("S", 3), ("PV", 1), ("CT", 0), ("PT", 2)] + ATT_END[:-1] + MLP_IN[:3] + MLP_IN[4:] + MLP_OUT



WORK_BANKS = {"XT": 2, "SM": 1, "MM": 1, "QK": 1, "VV": 1, "TR": 1, "S": 1, "PT": 1, "PV": 1, "CT": 1, "WO": 1, "NT": 1,
              "F1": 1, "F2": 1}
UPDATE_BANKS = ("SS", "TX", "NB", "NX", "WX")
UPD0, UPD1, GRAM0, GRAM1 = 4, 5, 6, 7


def bank_plan(steps):
    plan, held, turn, upd_turn = {}, set(), 0, 0
    for step in steps:
        kind = step[0]
        if kind == "GB":
            held |= {2 * step[1], 2 * step[1] + 1}
        elif kind == "EL":
            held -= {2 * step[1], 2 * step[1] + 1}
        elif kind == "DW" and step[1] == 0:
            held |= {0}
        elif kind == "MU" and step[1] == G_W0:
            held -= {0}
        elif kind == "OUT" and step[1] == 0:
            held |= {2, 3}
        elif kind == "OY":
            held -= {2, 3}
        elif kind in WORK_BANKS:
            plan[step] = []
            for _ in range(WORK_BANKS[kind]):
                while turn % 4 in held:
                    turn += 1
                plan[step].append(turn % 4)
                turn += 1
        elif kind in UPDATE_BANKS:
            plan[step] = [UPD0 + upd_turn % 2]
            upd_turn += 1
    return plan


def layer_kernel(nc, x, Wqkv, Wlr, Wm, bm, Ws, bs, Wo, w0, w1, w2, o_norm_g, qk_scale, qk_offset,
                 proj1, proj1_bias, proj2, proj2_bias, out):
    with ExitStack() as ctx:
        def sb(name, *shape):
            return ctx.enter_context(nc.sbuf_tensor(name, [P, *shape], F32))

        def share(whole, at, *shape):
            flat = whole[tuple([slice(None)] * len(whole.shape))]
            names = "abcdef"[:len(whole.shape) - 1]
            if len(names) > 1:
                flat = flat.rearrange(f"p {' '.join(names)} -> p ({' '.join(names)})")
            flat = flat[:, at:at + int(np.prod(shape))]
            names = "abcdef"[:len(shape)]
            if len(names) == 1:
                return flat
            return flat.rearrange(f"p ({' '.join(names)}) -> p {' '.join(names)}", **dict(zip(names, shape)))

        def sem(name):
            return ctx.enter_context(nc.semaphore(name))

        gram = ctx.enter_context(nc.psum_tensor("gram", [P, 2, 512], F32))
        upd = [ctx.enter_context(nc.psum_tensor(f"upd{n}", [P, 512], F32)) for n in range(2)]
        work = [ctx.enter_context(nc.psum_tensor(f"work{n}", [P, 2, 512], F32)) for n in range(2)]
        BANK = [work[0][:, 0, :], work[0][:, 1, :], work[1][:, 0, :], work[1][:, 1, :], upd[0][:, :], upd[1][:, :],
                gram[:, 0, :], gram[:, 1, :]]

        ident = sb("ident", P)
        ones_blk = sb("ones_blk", P)
        ones_avg = sb("ones_avg", HD)
        mask = sb("mask", 2 * P)
        mask_prev = sb("mask_prev", P)
        half = sb("half", 32)
        neg_half = sb("neg_half", 32)
        wqkv = sb("wqkv", KC, 3 * DIM)
        wsmall = sb("wsmall", KC, SMALL)
        small_bias = sb("small_bias", SMALL)
        wo = sb("wo", KC, DIM)
        p1T = sb("p1T", KC, HID)
        p2T = sb("p2T", HC, DIM)
        b1 = sb("b1", HC)
        b2 = sb("b2", DIM)
        g_raw = sb("g_raw", HD)
        g_half = sb("g_half", HD)
        qk_sc = sb("qk_sc", KC, 2)
        qk_of = sb("qk_of", KC, 2)
        row_norm = sb("row_norm", 3, 8)
        x_in = sb("x_in", BATCH, DIM)
        x_res = sb("x_res", BATCH, DIM)
        st1 = sb("st1", BATCH, 6)
        mv1 = sb("mv1", BATCH, 2)
        var1 = sb("var1", BATCH)
        rstd1 = sb("rstd1", BATCH)
        xnT = sb("xnT", KC, BATCH * P)
        small = sb("small", BATCH, SMALL)
        lr_neg = sb("lr_neg", BATCH, 12)
        lr_exp = sb("lr_exp", BATCH, 12)
        lr_log = sb("lr_log", BATCH, 12)
        lr = sb("lr", BATCH, 12)
        ms_t = sb("ms_t", BATCH, 8)
        ms = sb("ms", BATCH, 8)
        mm = sb("mm", 8)
        decayed = sb("decayed", 3, 8, HD)
        raw = sb("raw", BATCH, 3 * DIM)
        silu = sb("silu", BATCH, 3 * DIM)
        ssq = sb("ssq", BATCH, 8)
        nq = sb("nq", BATCH, 8)
        nqe = sb("nqe", BATCH, 8)
        rq = sb("rq", BATCH, 8)
        kl0 = sb("kl0", BATCH, NH, HD)
        kl2 = sb("kl2", BATCH, NH, HD)
        vl1 = sb("vl1", BATCH, NH, HD)
        aqT = sb("aqT", NAH, BATCH, P)
        akT = sb("akT", NAH, BATCH, 2, P)
        tttT = sb("tttT", 3, 2, BATCH, P)
        W = sb("W", 3, BATCH * 2, HD)
        WT02 = sb("WT02", BATCH, 2, 2, HD)
        W1T = sb("W1T", BATCH, 2, HD)
        out_ms = sb("out_ms", 2, BATCH, 2)
        out_v = sb("out_v", 2, BATCH, 2)
        out_rs = sb("out_rs", 2, BATCH, 2)
        out_f = sb("out_f", 2, BATCH, 2)
        y = sb("y", BATCH, NH, HD)
        M = sb("M", 3, 8, HD)
        m_ss = sb("m_ss", 3, 8)
        ss = sb("ss", 3, 8)
        fro = sb("fro", 3, 8)
        fro_e = sb("fro_e", 3, 8)
        rfro = sb("rfro", 3, 8)
        X = sb("X", 3, 8, HD)
        XT = sb("XT", 3, 8, HD)
        A = sb("A", 3, 8, HD)
        B = sb("B", 3, 8, HD)
        u_ss = sb("u_ss", 3, 8)
        u_n = sb("u_n", 3, 8)
        u_e = sb("u_e", 3, 8)
        u_r = sb("u_r", 3, 8)
        u_f = sb("u_f", 3, 8)
        masked = sb("masked", 2, 2, 2 * P)
        smax = sb("smax", BATCH, 2)
        nmax = sb("nmax", BATCH, 2)
        psums = sb("psums", BATCH, 2)
        rsums = sb("rsums", BATCH, 2)
        pT = sb("pT", 2, 2, 2, P)
        v_prev = sb("v_prev", BATCH, DIM)
        cT = sb("cT", 2, KC, P)
        st2 = sb("st2", BATCH, 6)
        mv2 = sb("mv2", BATCH, 2)
        var2 = sb("var2", BATCH)
        rstd2 = sb("rstd2", BATCH)
        x1 = sb("x1", BATCH, DIM)
        st3 = sb("st3", BATCH, 6)
        mv3 = sb("mv3", BATCH, 2)
        var3 = sb("var3", BATCH)
        rstd3 = sb("rstd3", BATCH)
        xn2T = sb("xn2T", KC, BATCH * P)
        h = sb("h", HC, BATCH * P)
        st4 = sb("st4", BATCH, 6)
        mv4 = sb("mv4", BATCH, 2)
        var4 = sb("var4", BATCH)
        rstd4 = sb("rstd4", BATCH)

        p1_raw, p2_raw = share(h, 0, HC, DIM), share(h, HC * DIM, KC, HID)
        gba_t, one_t, dxh, gms = (share(h, n * 1024, 2, 8, HD) for n in range(4))
        dsig, dgba = gms, dxh
        w_in = share(X, 0, 3, 2, HD)
        sg, dhbm = share(X, 0, 2, 8, HD), share(XT, 512, 2, 8, HD)
        gT = share(pT, 0, 2, 4, P)
        hidden = sb("hidden", 2, 8, HD)
        sq = share(hidden, 0, 2, 2 * DIM)
        dh = share(A, 0, 2, 2, 2, 2, HD)
        fw_t = share(B, 0, 2, 512)
        fw_s = fw_t
        out_sq = share(B, 0, 2, 8, HD)
        yg = y
        m_sq, u_sq, U, V = XT, B, A, decayed
        rows_a = sb("rows_a", BATCH, DIM)
        wo_n = f2 = f2_n = outb = rows_a
        rows_b = sb("rows_b", BATCH, DIM)
        xn = xn2 = comb = rows_b
        prob = masked
        qn = silu

        S = {name: Signal(sem("s_" + name), n) for name, n in RISES.items()}
        ld_qkv, ld_small, ld_misc, ld_w, ld_p1, ld_p2, ld_wo = (sem(n) for n in (
            "ld_qkv", "ld_small", "ld_misc", "ld_w", "ld_p1", "ld_p2", "ld_wo"))
        zeroed = sem("zeroed")
        consts = sem("consts")
        folded = sem("folded")
        w_sq0 = sem("w_sq0")
        w_ss0 = sem("w_ss0")
        norms = sem("norms")
        pT_ps = sem("pT_ps")
        pT_done = sem("pT_done")
        MISC = 16 * 7

        def wait_apart(eng, *waits):
            waits = [(sem_, n if isinstance(n, int) else eng.to_reg(n)) for sem_, n in filter(None, waits)]
            eng.wait_ge(consts, 1)
            for sem_, n in waits:
                eng.wait_ge(sem_, n)

        def bcast(ap, n):
            return ap.unsqueeze(len(ap.shape)).to_broadcast([*ap.shape, n])

        def rows(c):
            return x[:, bass.ts(c, CHUNK), :].rearrange("b p d -> p b d")

        block = ctx.enter_context(nc.Block())

        @block.sync
        def _(sp):
            sp.dma_start(x_in[:, :, :], rows(0)).then_inc(S["x_in"].sem, 16)
            sp.dma_start(wsmall[:, :, 0:12], Wlr.rearrange("(k p) n -> p k n", p=P)).then_inc(ld_small, 16)
            sp.dma_start(wsmall[:, :, 12:16], Wm.rearrange("(k p) n -> p k n", p=P)).then_inc(ld_small, 16)
            sp.dma_start(wsmall[:, :, 16:20], Ws.rearrange("(k p) n -> p k n", p=P)).then_inc(ld_small, 16)
            sp.dma_start(wqkv[:, :, :], Wqkv.rearrange("(k p) n -> p k n", p=P)).then_inc(ld_qkv, 16)
            sp.dma_start(small_bias[:, 12:16], bm.partition_broadcast(P)).then_inc(ld_misc, 16)
            sp.dma_start(small_bias[:, 16:20], bs.partition_broadcast(P)).then_inc(ld_misc, 16)
            sp.dma_start(g_raw[:, :], o_norm_g.partition_broadcast(P)).then_inc(ld_misc, 16)
            sp.dma_start(b2[:, :], proj2_bias.partition_broadcast(P)).then_inc(ld_misc, 16)
            sp.dma_start(qk_sc[:, :, :], qk_scale.rearrange("(k p) n -> p k n", p=P)).then_inc(ld_misc, 16)
            sp.dma_start(qk_of[:, :, :], qk_offset.rearrange("(k p) n -> p k n", p=P)).then_inc(ld_misc, 16)
            sp.dma_start(b1[:, :], proj1_bias.rearrange("(k p) -> p k", p=P), allow_slow_non_contiguous=True).then_inc(ld_misc, 16)
            sp.dma_start(wo[:, :, :], Wo.rearrange("(k p) n -> p k n", p=P)).then_inc(ld_wo, 16)
            with sp.Fori(0, CHUNKS - 1) as c:
                sp.wait_ge(*S["x_res"](c, 1))
                sp.wait_ge(*S["xn"](c, 1))
                sp.dma_start(x_in[:, :, :], rows(c + 1)).then_inc(S["x_in"].sem, 16)
                for b in range(BATCH):
                    sp.wait_ge(*S["outb"](c, b + 1))
                    sp.dma_start(out[b, bass.ts(c, CHUNK), :], outb[:, b, :]).then_inc(S["stored"].sem, 16)
            c = CHUNKS - 1
            for b in range(BATCH):
                sp.wait_ge(*S["outb"](c, b + 1))
                sp.dma_start(out[b, bass.ts(c, CHUNK), :], outb[:, b, :]).then_inc(S["stored"].sem, 16)
            sp.wait_ge(*S["stored"](CHUNKS, 0))

        @block.tensor
        def _(pe):
            owner = {}

            def free(bank, signal, c, n, covered_by=()):
                last = owner.get(bank)
                owner[bank] = (signal, c, n)
                return None if last is None or last[0] in covered_by else S[last[0]](*last[1:])

            def take(bank, signal, c, n, covered_by=()):
                last = free(bank, signal, c, n, covered_by)
                if last is not None:
                    pe.wait_ge(*last)
                return BANK[bank]

            def all_read_out(c):
                for name in ("el", "dh", "mom", "gT", "y", "masked", "pT", "comb", "cT", "wo_n", "xn2T", "h", "f2", "ss",
                             "XT", "A", "B", "X"):
                    pe.wait_ge(*S[name](c, 0))
                for name in ("xnT", "small", "mm", "qk_raw", "v_raw", "att_T", "ttt_T", "WT"):
                    pe.wait_ge(*S[name](c + 1, 0))
                owner.clear()

            def XT_(bank, c):
                pe.wait_ge(*S["xn"](c, 1))
                for k in range(KC):
                    ps = take(bank[k], "xnT", c, k + 1)
                    for b in range(BATCH):
                        mm_ = pe.transpose(ps[:, b * P:(b + 1) * P], xn[:, b, k * P:(k + 1) * P], ident[:, :])
                    mm_.then_inc(S["xT_ps"].sem, 1)

            def SM(bank, c):
                pe.wait_ge(ld_small, 48)
                ps = take(bank[0], "small", c, 1)
                pe.wait_ge(*S["xnT"](c, 2))
                for b in range(BATCH):
                    for k in range(KC):
                        mm_ = pe.matmul(ps[:, b * SMALL:(b + 1) * SMALL], xnT[:, k, b * P:(b + 1) * P], wsmall[:, k, :],
                                        start=(k == 0), stop=(k == KC - 1))
                mm_.then_inc(S["small_ps"].sem, 1)

            def MM(bank, c):
                ps = BANK[bank[0]]
                wait_apart(pe, free(bank[0], "mm", c, 1), S["ms"](c, 1))
                for i in range(2):
                    mm_ = pe.matmul(ps[64 * i:64 * i + 64, 0:8], ones_avg[:, :],
                                    ms[:, :, 2 * i:2 * i + 2], start=True, stop=True)
                mm_.then_inc(S["mm_ps"].sem, 1)

            def QK(bank, c, b):
                pe.wait_ge(ld_qkv, 16)
                ps = take(bank[0], "qk_raw", c, b + 1)
                pe.wait_ge(*S["xnT"](c, 2))
                for k in range(KC):
                    mm_ = pe.matmul(ps, xnT[:, k, b * P:(b + 1) * P], wqkv[:, k, 0:512], start=(k == 0), stop=(k == KC - 1))
                mm_.then_inc(S["qk_ps"].sem, 1)

            def VV(bank, c, b):
                ps = take(bank[0], "v_raw", c, b + 1)
                for k in range(KC):
                    mm_ = pe.matmul(ps[:, 0:256], xnT[:, k, b * P:(b + 1) * P], wqkv[:, k, 512:768],
                                    start=(k == 0), stop=(k == KC - 1))
                mm_.then_inc(S["v_ps"].sem, 1)

            def TR(bank, c, u):
                if u < 4:
                    ps = take(bank[0], "att_T", c, u + 1)
                    pe.wait_ge(*S["qk_raw"](c, 4))
                else:
                    ps = take(bank[0], "ttt_T", c, u - 3)
                    pe.wait_ge(*S["qn"](c, 4))
                for b in range(BATCH):
                    if u < 4:
                        src = raw[:, b, u * P:(u + 1) * P]
                    elif u < 8:
                        src = qn[:, b, (u - 4) * P:(u - 3) * P]
                    else:
                        src = silu[:, b, 512 + (u - 8) * P:512 + (u - 7) * P]
                    mm_ = pe.transpose(ps[:, b * P:(b + 1) * P], src, ident[:, :])
                mm_.then_inc(S["tr_ps"].sem, 1)

            def GB(c, bp):
                wait_apart(pe, free(2 * bp, "el", c, bp + 1), free(2 * bp + 1, "el", c, bp + 1))
                for b2_ in range(2):
                    for j in range(2):
                        for r in range(2):
                            b = 2 * bp + b2_
                            at = (b2_ * 2 + j) * P
                            mm_ = pe.matmul(BANK[2 * bp + r][:, at:at + P], tttT[64 * r:64 * r + 64, 1, j, b, :],
                                            WT02[64 * r:64 * r + 64, b, j, :, :], start=True, stop=True)
                mm_.then_inc(S["gba_ps"].sem, 1)

            def DH(c):
                wait_apart(pe, free(GRAM0, "dh", c, 1, ("A", "dh")), free(GRAM1, "dh", c, 1))
                for b in range(BATCH):
                    for j in range(2):
                        for r in range(2):
                            at = ((b // 2) * 4 + j * 2 + b % 2) * HD
                            mm_ = pe.matmul(BANK[GRAM0 + r][:, at:at + HD], tttT[64 * r:64 * r + 64, 2, j, b, :],
                                            W[64 * r:64 * r + 64, G_W1, 2 * b + j, :], start=True, stop=True)
                mm_.then_inc(S["dh_ps"].sem, 1)

            def FW(c, bp):
                wait_apart(pe, free(UPD0, "gT", c, bp + 1, ("gT",)), free(UPD1, "gT", c, bp + 1))
                for ps, kind in ((BANK[UPD0], 0), (BANK[UPD1], 1)):
                    for b2_ in range(2):
                        for j in range(2):
                            for r in range(2):
                                b = 2 * bp + b2_
                                at = (b2_ * 2 + j) * P
                                mm_ = pe.matmul(ps[64 * r:64 * r + 64, at:at + P], WT02[64 * r:64 * r + 64, b, j, kind, :],
                                                tttT[64 * r:64 * r + 64, 0, j, b, :], start=True, stop=True)
                mm_.then_inc(S["fw_ps"].sem, 1)

            def OUT(c, bp):
                if bp == 0:
                    wait_apart(pe, free(2, "y", c, 1), free(3, "y", c, 1), S["gT"](c, 1))
                else:
                    wait_apart(pe, S["gT"](c, 2))
                for b2_ in range(2):
                    for j in range(2):
                        for r in range(2):
                            b = 2 * bp + b2_
                            at = (2 * b + j) * HD
                            mm_ = pe.matmul(BANK[2 + r][:, at:at + HD], gT[64 * r:64 * r + 64, bp, 2 * b2_ + j, :],
                                            W1T[64 * r:64 * r + 64, b, j, :], start=True, stop=True)
                mm_.then_inc(S["out_ps"].sem, 1)

            def DW(c, bp):
                for g, bank, left, right, ready in ((G_W1, GRAM0, vl1, hidden, "el"), (G_W2, GRAM1, dhbm, kl2, "dhbm"),
                                                    (G_W0, 0, dgba, kl0, "dgba")):
                    wait_apart(pe, free(bank, "mom", c, g + 1) if bp == 0 else None, S[ready](c, bp + 1))
                    for b2_ in range(2):
                        b = 2 * bp + b2_
                        for hd in range(NH):
                            i, j = divmod(hd, 2)
                            slot = (hd % 2) * 4 + b2_ * 2 + hd // 2
                            lhs = left[:, b, 2 * j + i, :] if g == G_W1 else left[:, bp, slot, :]
                            rhs = right[:, bp, slot, :] if g == G_W1 else right[:, b, hd, :]
                            mm_ = pe.matmul(BANK[bank][64 * i:64 * i + 64, (2 * b + j) * HD:(2 * b + j + 1) * HD], lhs, rhs,
                                            start=True, stop=True)
                    if bp == 1:
                        mm_.then_inc(S["dw_ps"].sem, 1)

            def SS(bank, c, g):
                ps = take(bank[0], "ss", c, g + 1)
                pe.wait_ge(*S["mom_ss"](c, g + 1))
                pe.matmul(ps[:, 0:8], ones_blk[:, :], m_ss[:, g, :], start=True, stop=True).then_inc(S["ss_ps"].sem, 1)

            def TX(bank, c, it, g):
                ps = take(bank[0], "XT", c, 3 * it + g + 1, ("X",) if it else ())
                if it == 0:
                    pe.wait_ge(*S["x0"](c, g + 1))
                else:
                    pe.wait_ge(*S["X"](c, 3 * (it - 1) + g + 1))
                for b in range(BATCH):
                    mm_ = pe.transpose(ps[:, b * P:(b + 1) * P], X[:, g, 2 * b:2 * b + 2, :], ident[:, :])
                mm_.then_inc(S["xt_ps"].sem, 1)

            def NA(c, it, g):
                wait_apart(pe, free(GRAM0, "A", c, 3 * it + g + 1, ("mom", "A")), free(GRAM1, "A", c, 3 * it + g + 1),
                           S["XT"](c, 3 * it + g + 1))
                for b in range(BATCH):
                    for i, j in ((0, 0), (1, 1), (0, 1), (1, 0)):
                        half_ = XT[64 * j:64 * j + 64, g, 2 * b + i, :]
                        mm_ = pe.matmul(BANK[GRAM0 + j][64 * i:64 * i + 64, b * HD:(b + 1) * HD], half_, half_,
                                        start=True, stop=True)
                mm_.then_inc(S["a_ps"].sem, 1)

            def NB(bank, c, it, g):
                ps = BANK[bank[0]]
                wait_apart(pe, free(bank[0], "B", c, 3 * it + g + 1), S["A"](c, 3 * it + g + 1))
                for slot in range(8):
                    for i in range(2):
                        a = A[64 * i:64 * i + 64, g, slot, :]
                        mm_ = pe.matmul(ps[64 * i:64 * i + 64, slot * HD:(slot + 1) * HD], a, a, start=True, stop=True)
                mm_.then_inc(S["b_ps"].sem, 1)

            def NX(bank, c, it, g):
                ps = BANK[bank[0]]
                wait_apart(pe, free(bank[0], "X", c, 3 * it + g + 1, ("B",)), S["B"](c, 3 * it + g + 1))
                for slot in range(8):
                    for i in range(2):
                        mm_ = pe.matmul(ps[64 * i:64 * i + 64, slot * HD:(slot + 1) * HD], B[64 * i:64 * i + 64, g, slot, :],
                                        X[64 * i:64 * i + 64, g, slot, :], start=True, stop=True)
                mm_.then_inc(S["x_ps"].sem, 1)

            def WX(bank, c, g):
                ps = take(bank[0], "WT", c, g + 1)
                pe.wait_ge(*S["W"](c, g + 1))
                for b in range(BATCH):
                    mm_ = pe.transpose(ps[:, b * P:(b + 1) * P], W[:, g, 2 * b:2 * b + 2, :], ident[:, :])
                mm_.then_inc(S["w_ps"].sem, 1)

            def SC(bank, c, b):
                ps = take(bank[0], "masked", c, b + 1)
                if b == 0:
                    pe.wait_ge(*S["att_T"](c + 1, 0))
                    pe.wait_ge(*S["k_prev"](c, 0))
                for hd in range(NAH):
                    mm_ = pe.matmul(ps[:, hd * 256:(hd + 1) * 256], aqT[:, hd, b, :], akT[:, hd, b, :, :], start=True, stop=True)
                mm_.then_inc(S["s_ps"].sem, 1)

            def PT(bank, c, b):
                ps = take(bank[0], "pT", c, b + 1)
                pe.wait_ge(*S["prob"](c, b + 1))
                for n in range(4):
                    mm_ = pe.transpose(ps[:, n * P:(n + 1) * P], prob[:, b % 2, n // 2, (n % 2) * P:(n % 2 + 1) * P], ident[:, :])
                mm_.then_inc(S["pt_ps"].sem, 1)

            def PV(bank, c, b):
                ps = take(bank[0], "comb", c, b + 1, ("pT",))
                if b == 0:
                    pe.wait_ge(*S["v_prev"](c, 0))
                pe.wait_ge(*S["pT"](c, b + 1))
                for hd in range(NAH):
                    for n in range(2):
                        val = v_prev[:, b, hd * P:(hd + 1) * P] if n == 0 else raw[:, b, 512 + hd * P:512 + (hd + 1) * P]
                        mm_ = pe.matmul(ps[:, hd * P:(hd + 1) * P], pT[:, b % 2, hd, n, :], val, start=(n == 0), stop=(n == 1))
                mm_.then_inc(S["pv_ps"].sem, 1)

            def CT(bank, c, b):
                ps = take(bank[0], "cT", c, b + 1, ("comb",))
                pe.wait_ge(*S["comb"](c, b + 1))
                for k in range(KC):
                    mm_ = pe.transpose(ps[:, k * P:(k + 1) * P], comb[:, b, k * P:(k + 1) * P], ident[:, :])
                mm_.then_inc(S["ct_ps"].sem, 1)

            def WO(bank, c, b):
                pe.wait_ge(ld_wo, 16)
                ps = take(bank[0], "wo_n", c, b + 1, ("cT",))
                pe.wait_ge(*S["cT"](c, b + 1))
                for k in range(KC):
                    mm_ = pe.matmul(ps[:, 0:DIM], cT[:, b % 2, k, :], wo[:, k, :], start=(k == 0), stop=(k == KC - 1))
                mm_.then_inc(S["wo_ps"].sem, 1)

            def NT(bank, c, b):
                ps = take(bank[0], "xn2T", c, b + 1)
                pe.wait_ge(*S["xn2"](c, b + 1))
                for k in range(KC):
                    mm_ = pe.transpose(ps[:, k * P:(k + 1) * P], xn2[:, b, k * P:(k + 1) * P], ident[:, :])
                mm_.then_inc(S["nt_ps"].sem, 1)

            def F1(bank, c, n):
                ps = take(bank[0], "h", c, n + 1, ("xn2T",) if n == 0 else ())
                if n == 0:
                    pe.wait_ge(*S["xn2T"](c, 4))
                for k in range(KC):
                    mm_ = pe.matmul(ps, p1T[:, k, n * P:(n + 1) * P], xn2T[:, k, :], start=(k == 0), stop=(k == KC - 1))
                mm_.then_inc(S["f1_ps"].sem, 1)

            def F2(bank, c, b):
                ps = take(bank[0], "f2", c, b + 1, ("h",) if b == 0 else ())
                if b == 0:
                    pe.wait_ge(*S["h"](c, 8))
                for n in range(HC):
                    mm_ = pe.matmul(ps[:, 0:DIM], h[:, n, b * P:(b + 1) * P], p2T[:, n, :], start=(n == 0), stop=(n == HC - 1))
                mm_.then_inc(S["f2_ps"].sem, 1)

            of_next = {"XT": XT_, "SM": SM, "MM": MM, "QK": QK, "VV": VV, "TR": TR, "WX": WX}
            of_this = {"GB": GB, "DH": DH, "FW": FW, "OUT": OUT, "DW": DW, "SS": SS, "TX": TX, "NA": NA, "NB": NB, "NX": NX,
                       "S": SC, "PT": PT, "PV": PV, "CT": CT, "WO": WO, "NT": NT, "F1": F1, "F2": F2}

            def run(steps, c):
                plan = bank_plan(steps)
                for step in steps:
                    kind, *arg = step
                    bank = [plan[step]] if step in plan else []
                    if kind in of_next:
                        of_next[kind](*bank, c + 1, *arg)
                    elif kind in of_this:
                        of_this[kind](*bank, c, *arg)

            pe.wait_ge(consts, 1)
            for g in range(3):
                WX([UPD0 + g % 2], 0, g)
            run(FIRST, -1)
            all_read_out(0)
            done = [0]
            for src, wait in ((p1_raw, ld_p1), (p2_raw, ld_p2)):
                pe.wait_ge(wait, 16)
                for n in range(4):
                    if done[0] >= 4:
                        pe.wait_ge(pT_done, done[0] - 3)
                    ps = BANK[n]
                    for q in range(4):
                        if src is p1_raw:
                            blk = p1_raw[:, 4 * (n % 2) + q, (n // 2) * P:(n // 2 + 1) * P]
                        else:
                            col = (2 * n + q // 2) * P
                            blk = p2_raw[:, q % 2, col:col + P]
                        mm_ = pe.transpose(ps[:, q * P:(q + 1) * P], blk, ident[:, :])
                    mm_.then_inc(pT_ps, 1)
                    done[0] += 1
            pe.wait_ge(pT_done, 8)

            with pe.Fori(0, CHUNKS - 1) as c:
                all_read_out(c)
                run(BODY, c)
            all_read_out(CHUNKS - 1)
            run(LAST, CHUNKS - 1)

        @block.scalar
        def _(act):
            def copy(dst, src):
                return act.activation(dst, src, ACT.Copy)

            def XT_(bank, c):
                for k in range(KC):
                    act.wait_ge(*S["xT_ps"](c, k + 1))
                    if k == 0:
                        act.wait_ge(*S["v_ps"](c, 0))
                    copy(xnT[:, k, :], BANK[bank[k]]).then_inc(S["xnT"].sem, 1)

            def SP(c):
                act.wait_ge(*S["lr_neg"](c, 1))
                act.activation(lr_exp[:, :, :], lr_neg[:, :, :], ACT.Exp).then_inc(S["lr_exp"].sem, 1)
                act.wait_ge(*S["lr_exp"](c, 1))
                act.activation(lr_log[:, :, :], lr_exp[:, :, :], ACT.Ln, bias=1.0).then_inc(S["lr_log"].sem, 1)

            def MS(c):
                act.preload_act_table_set("gelu_and_others")
                act.wait_ge(*S["small"](c, 1))
                act.activation(ms_t[:, :, :], small[:, :, 12:20], ACT.Tanh, scale=0.5).then_inc(S["ms_tanh"].sem, 1)

            def QK(bank, c, b):
                act.wait_ge(*S["qk_ps"](c, b + 1))
                act.wait_ge(*S["tr_ps"](c, 0))
                act.wait_ge(*S["silu"](c, 0))
                copy(raw[:, b, 0:512], BANK[bank[0]]).then_inc(S["qk_raw"].sem, 1)

            def SI(c, b):
                act.wait_ge(*S["v_raw"](c, b + 1))
                act.wait_ge(*S["qk_raw"](c, b + 1))
                act.wait_ge(*S["klv"](c, 0))
                act.wait_ge(*S["tr_ps"](c, 0))
                act.activation(silu[:, b, 0:512], raw[:, b, 0:512], ACT.Tanh, scale=0.5)
                act.activation(silu[:, b, 512:768].rearrange("p (j r d) -> p r j d", j=2, r=2),
                               raw[:, b, 512:768].rearrange("p (r j d) -> p r j d", j=2, r=2), ACT.Tanh, scale=0.5)\
                    .then_inc(S["sig"].sem, 1)

            def TR(bank, c, u):
                ps = BANK[bank[0]]
                if u >= 4:
                    return
                kind, hd = divmod(u, 2)
                act.wait_ge(*S["tr_ps"](c, u + 1))
                if kind == 0:
                    act.wait_ge(*S["s_ps"](c, 0))
                    dst = aqT[:, hd, :, :]
                else:
                    act.wait_ge(*S["k_prev"](c, 0))
                    dst = akT[:, hd, :, 1, :]
                act.activation(dst, ps.rearrange("p (b t) -> p b t", b=BATCH), ACT.Identity,
                               bias=qk_of[:, hd, kind:kind + 1], scale=qk_sc[:, hd, kind:kind + 1]).then_inc(S["att_T"].sem, 1)

            def GB(c, bp):
                act.wait_ge(*S["gba_ps"](c, bp + 1))
                act.wait_ge(*S["dgba"](c, 0))
                act.wait_ge(*S["one_t"](c, 0))
                gba = work[bp][:, :, :].rearrange("p r (s k d) -> p (r s) k d", s=4, k=2)[:, :, 0, :]
                act.activation(gba_t[:, bp, :, :], gba, ACT.Tanh, scale=0.5).then_inc(S["gba_tanh"].sem, 1)

            def DH(c):
                act.wait_ge(*S["dh_ps"](c, 1))
                act.wait_ge(*S["dhbm"](c, 0))
                for r in range(2):
                    last = copy(dh[:, :, :, :, r, :].rearrange("p x j y d -> p (x j y) d"),
                                gram[:, r, :].rearrange("p (s d) -> p s d", d=HD))
                last.then_inc(S["dh"].sem, 1)

            def FW(c, bp):
                act.wait_ge(*S["fw_ps"](c, bp + 1))
                act.wait_ge(*S["fw_silu"](c, 0))
                act.activation(fw_t[:, bp, :], upd[0][:, :], ACT.Tanh, scale=0.5).then_inc(S["fw_tanh"].sem, 1)

            def OE(c):
                act.wait_ge(*S["out_ps"](c, 2))
                for r in range(2):
                    last = act.activation(out_sq[:, r, :, :], work[1][:, r, :].rearrange("p (s d) -> p s d", d=HD), ACT.Square)
                last.then_inc(S["out_sq"].sem, 1)

            def MU(c, g):
                act.wait_ge(*S["mom"](c, g + 1))
                act.activation(m_sq[:, g, :, :], M[:, g, :, :], ACT.Square).then_inc(S["mom_sq"].sem, 1)

            def TX(bank, c, it, g):
                act.wait_ge(*S["xt_ps"](c, 3 * it + g + 1))
                copy(XT[:, g, :, :], BANK[bank[0]].rearrange("p (s d) -> p s d", d=HD)).then_inc(S["XT"].sem, 1)

            def NA(c, it, g):
                act.wait_ge(*S["a_ps"](c, 3 * it + g + 1))
                if it:
                    act.wait_ge(*S["B"](c, 3 * (it - 1) + g + 1))
                copy(A[:, g, :, :].rearrange("p (b j) d -> p j b d", j=2),
                     gram[:, :, 0:256].rearrange("p j (b d) -> p j b d", d=HD)).then_inc(S["A"].sem, 1)

            def RN(c, g):
                act.wait_ge(*S["X"](c, 3 * (NIT - 1) + g + 1))
                act.activation(u_sq[:, g, :, :], U[:, g, :, :], ACT.Square).then_inc(S["u_sq"].sem, 1)

            def WX(bank, c, g):
                act.wait_ge(*S["w_ps"](c, g + 1))
                ps = BANK[bank[0]].rearrange("p (b j d) -> p b j d", b=BATCH, j=2)
                if g == G_W1:
                    act.wait_ge(*S["out_ps"](c, 0))
                    dst = W1T[:, :, :, :]
                else:
                    act.wait_ge(*S["fw_ps"](c, 0))
                    act.wait_ge(*S["gba_ps"](c, 0))
                    dst = WT02[:, :, :, 0 if g == G_W0 else 1, :]
                copy(dst, ps).then_inc(S["WT"].sem, 1)

            def SC(c, b):
                if b == 0:
                    act.preload_act_table_set("natural_log_exp_and_others")
                act.wait_ge(*S["neg_max"](c, b + 1))
                if b >= 2:
                    act.wait_ge(*S["pt_ps"](c, b - 1))
                else:
                    act.wait_ge(*S["pt_ps"](c, 0))
                    act.wait_ge(*S["psum_r"](c, 0))
                for hd in range(NAH):
                    last = act.activation(prob[:, b % 2, hd, :], masked[:, b % 2, hd, :], ACT.Exp, bias=nmax[:, b, hd:hd + 1],
                                          scale=SCALE, accum_out=psums[:, b, hd:hd + 1])
                last.then_inc(S["prob"].sem, 1)

            def PT(bank, c, b):
                act.wait_ge(*S["pt_ps"](c, b + 1))
                if b >= 2:
                    act.wait_ge(*S["pv_ps"](c, b - 1))
                copy(pT[:, b % 2, :, :, :].rearrange("p h n t -> p (h n t)"), BANK[bank[0]]).then_inc(S["pT"].sem, 1)

            def CT(bank, c, b):
                act.wait_ge(*S["ct_ps"](c, b + 1))
                if b >= 2:
                    act.wait_ge(*S["wo_ps"](c, b - 1))
                copy(cT[:, b % 2, :, :].rearrange("p k t -> p (k t)"), BANK[bank[0]][:, 0:256]).then_inc(S["cT"].sem, 1)

            def NT(bank, c, b):
                act.wait_ge(*S["nt_ps"](c, b + 1))
                copy(xn2T[:, :, b * P:(b + 1) * P], BANK[bank[0]][:, 0:256].rearrange("p (k t) -> p k t", k=KC))\
                    .then_inc(S["xn2T"].sem, 1)

            def F1(bank, c, n):
                act.wait_ge(*S["f1_ps"](c, n + 1))
                if n == 0:
                    act.wait_ge(*S["f2_ps"](c, 0))
                act.activation(h[:, n, :], BANK[bank[0]], ACT.Gelu, bias=b1[:, n:n + 1]).then_inc(S["h"].sem, 1)

            of_next = {"XT": XT_, "SP": SP, "MS": MS, "QK": QK, "SI": SI, "TR": TR, "WX": WX}
            of_this = {"GB": GB, "DH": DH, "FW": FW, "OE": OE, "MU": MU, "TX": TX, "NA": NA, "RN": RN, "S": SC, "PT": PT,
                       "CT": CT, "NT": NT, "F1": F1}
            READS = ("XT", "QK", "TR", "WX", "TX", "PT", "CT", "NT", "F1")

            def run(steps, c):
                plan = bank_plan(steps)
                for step in steps:
                    kind, *arg = step
                    bank = [plan[step]] if kind in READS else []
                    if kind in of_next:
                        of_next[kind](*bank, c + 1, *arg)
                    elif kind in of_this:
                        of_this[kind](*bank, c, *arg)

            for n, w in enumerate((w1, w2, w0)):
                for i in range(2):
                    act.dma_start(w_in[64 * i:64 * i + 64, n, :, :], w[2 * i:2 * i + 2, :, :].rearrange("j r d -> r j d"))\
                        .then_inc(ld_w, 16)
            act.dma_start(p1_raw[:, :, :], proj1.rearrange("(n p) e -> p n e", p=P)).then_inc(ld_p1, 16)
            act.dma_start(p2_raw[:, :, :], proj2.rearrange("(k p) n -> p k n", p=P)).then_inc(ld_p2, 16)
            act.preload_act_table_set("natural_log_exp_and_others")
            act.wait_ge(consts, 1)
            act.wait_ge(ld_misc, MISC)
            act.wait_ge(*S["W"](0, 3))
            for g in range(3):
                last = act.activation(u_sq[:, g, :, :], W[:, g, :, :], ACT.Square)
            last.then_inc(w_sq0, 1)
            for g in range(3):
                WX([UPD0 + g % 2], 0, g)
            run(FIRST, -1)
            for n in range(8):
                act.wait_ge(pT_ps, n + 1)
                ps = BANK[n % 4]
                if n < 4:
                    last = copy(p1T[:, n // 2, (n % 2) * 512:(n % 2 + 1) * 512], ps)
                else:
                    last = copy(p2T[:, 2 * (n - 4):2 * (n - 4) + 2, :].rearrange("p a b -> p (a b)"), ps)
                last.then_inc(pT_done, 1)
            with act.Fori(0, CHUNKS - 1) as c:
                run(BODY, c)
            run(LAST, CHUNKS - 1)

        @block.vector
        def _(dve):
            def stt(out_, in0, scalar, in1, op0, op1):
                return dve.scalar_tensor_tensor(out=out_, in0=in0, scalar=scalar, in1=in1, op0=op0, op1=op1)

            def LN1(c):
                dve.wait_ge(*S["x_in"](c, 16))
                dve.wait_ge(*S["xT_ps"](c, 0))
                for b in range(BATCH):
                    last = dve.bn_stats(st1[:, b, :], x_in[:, b, :])
                last.then_inc(S["ln1_stats"].sem, 1)
                wait_apart(dve, S["ln1_stats"](c, 1))
                for b in range(BATCH):
                    last = dve.bn_aggr(mv1[:, b, :], st1[:, b, :])
                last.then_inc(S["ln1_mv"].sem, 1)
                dve.wait_ge(*S["ln1_rstd"](c, 1))
                for b in range(BATCH):
                    last = dve.tensor_scalar(xn[:, b, :], x_in[:, b, :], mv1[:, b, 0:1], rstd1[:, b:b + 1],
                                             ALU.subtract, ALU.mult)
                last.then_inc(S["xn"].sem, 1)

            def SM(bank, c):
                dve.wait_ge(*S["small_ps"](c, 1))
                dve.wait_ge(*S["ms"](c, 0))
                dve.wait_ge(*S["lr"](c, 0))
                dve.tensor_tensor(small[:, :, :], BANK[bank[0]][:, 0:BATCH * SMALL].rearrange("p (b n) -> p b n", b=BATCH),
                                  small_bias[:, :].unsqueeze(1).to_broadcast([P, BATCH, SMALL]), ALU.add)\
                    .then_inc(S["small"].sem, 1)
                dve.wait_ge(*S["small"](c, 1))
                z = small[:, :, 0:12]
                stt(lr_neg[:, :, :], z, -1.0, z, ALU.mult, ALU.min).then_inc(S["lr_neg"].sem, 1)

            def SP(c):
                dve.wait_ge(*S["lr_log"](c, 1))
                dve.wait_ge(*S["klv"](c, 0))
                stt(lr[:, :, :], small[:, :, 0:12], 0.0, lr_log[:, :, :], ALU.max, ALU.add).then_inc(S["lr"].sem, 1)

            def MS(c):
                dve.wait_ge(*S["ms_tanh"](c, 1))
                dve.wait_ge(*S["out_f"](c, 0))
                dve.wait_ge(*S["mm_ps"](c, 0))
                dve.tensor_scalar(ms[:, :, 0:4], ms_t[:, :, 0:4], 1.0, None, ALU.add)
                stt(ms[:, :, 4:8], ms_t[:, :, 4:8], 1.0, small[:, :, 16:20], ALU.add, ALU.mult).then_inc(S["ms"].sem, 1)

            def MM(bank, c):
                dve.wait_ge(*S["mm_ps"](c, 1))
                dve.wait_ge(*S["decayed"](c, 0))
                dve.tensor_copy(mm[:, :], BANK[bank[0]][:, 0:8]).then_inc(S["mm"].sem, 1)

            def VV(bank, c, b):
                dve.wait_ge(*S["v_ps"](c, b + 1))
                dve.wait_ge(*S["v_prev"](c, 0))
                dve.tensor_copy(raw[:, b, 512:768], BANK[bank[0]][:, 0:256]).then_inc(S["v_raw"].sem, 1)

            def SI(c, b):
                dve.wait_ge(*S["sig"](c, b + 1))
                dve.wait_ge(*S["klv"](c, 0))
                dve.wait_ge(*S["tr_ps"](c, 0))
                stt(silu[:, b, 0:512], silu[:, b, 0:512], 1.0, raw[:, b, 0:512], ALU.add, ALU.mult)
                th = silu[:, b, 512:768].rearrange("p (j r d) -> p j r d", j=2, r=2)
                val = raw[:, b, 512:768].rearrange("p (r j d) -> p j r d", j=2, r=2)
                for j in range(2):
                    last = stt(th[:, j, :, :], th[:, j, :, :], 1.0, val[:, j, :, :], ALU.add, ALU.mult)
                last.then_inc(S["silu"].sem, 1)

            def NQ(c, b):
                dve.wait_ge(*S["sq"](c, b + 1))
                dve.tensor_reduce(ssq[:, b, :], sq[:, b % 2, :].rearrange("p (h d) -> p h d", d=HD), AX.X, ALU.add)\
                    .then_inc(S["ssq"].sem, 1)
                dve.wait_ge(*S["nq"](c, b + 1))
                dve.tensor_scalar(nqe[:, b, :], nq[:, b, :], 2.0e-5, None, ALU.add).then_inc(S["nq_eps"].sem, 1)
                dve.wait_ge(*S["nq_eps"](c, b + 1))
                dve.reciprocal(rq[:, b, :], nqe[:, b, :]).then_inc(S["rq"].sem, 1)

            def TR(bank, c, u):
                ps = BANK[bank[0]]
                if u < 4:
                    return
                kind, j = divmod(u - 4, 2)
                dve.wait_ge(*S["tr_ps"](c, u + 1))
                if u == 4:
                    dve.wait_ge(*S["fw_ps"](c, 0))
                    dve.wait_ge(*S["gba_ps"](c, 0))
                    dve.wait_ge(*S["dh_ps"](c, 0))
                dve.tensor_copy(tttT[:, kind, j, :, :].rearrange("p b t -> p (b t)"), ps).then_inc(S["ttt_T"].sem, 1)

            def EL(c, bp):
                both = work[bp][:, :, :].rearrange("p r (s k d) -> p (r s) k d", s=4, k=2)
                gba, hbm = both[:, :, 0, :], both[:, :, 1, :]
                dhs = dh[:, bp, :, :, :, :].rearrange("p r y j d -> p (r y j) d")
                dve.wait_ge(*S["gba_tanh"](c, bp + 1))
                if bp == 0:
                    dve.wait_ge(*S["dhbm"](c, 0))
                    dve.wait_ge(*S["dw_ps"](c, 0))
                stt(sg[:, bp, :, :], gba_t[:, bp, :, :], 1.0, gba, ALU.add, ALU.mult).then_inc(S["sg"].sem, 1)
                dve.wait_ge(*S["dh"](c, 1))
                dve.tensor_tensor(dxh[:, bp, :, :], dhs, hbm, ALU.mult)
                dve.wait_ge(*S["sg"](c, bp + 1))
                dve.tensor_tensor(hidden[:, bp, :, :], sg[:, bp, :, :], hbm, ALU.mult)
                stt(gms[:, bp, :, :], sg[:, bp, :, :], -0.5, gba, ALU.mult, ALU.add).then_inc(S["el"].sem, 1)

            def ELB(c, bp):
                dve.wait_ge(*S["one_t"](c, bp + 1))
                dve.wait_ge(*S["el"](c, bp + 1))
                stt(dsig[:, bp, :, :], gms[:, bp, :, :], 1.0, one_t[:, bp, :, :], ALU.add, ALU.mult).then_inc(S["dsig"].sem, 1)
                dve.wait_ge(*S["dsig"](c, bp + 1))
                dve.tensor_tensor(dgba[:, bp, :, :], dxh[:, bp, :, :], dsig[:, bp, :, :], ALU.mult).then_inc(S["dgba"].sem, 1)

            def FE(c, bp):
                dve.wait_ge(*S["fw_tanh"](c, bp + 1))
                stt(fw_s[:, bp, :], fw_t[:, bp, :], 1.0, upd[0][:, :], ALU.add, ALU.mult).then_inc(S["fw_silu"].sem, 1)
                dve.wait_ge(*S["fw_silu"](c, bp + 1))
                dve.wait_ge(*S["out_ps"](c, 0))
                dve.tensor_tensor(gT[:, bp, :, :].rearrange("p s t -> p (s t)"), fw_s[:, bp, :], upd[1][:, :], ALU.mult)\
                    .then_inc(S["gT"].sem, 1)

            def OE(c):
                dve.wait_ge(*S["out_sq"](c, 1))
                dve.tensor_reduce(out_ms[:, :, :, :].rearrange("p r b j -> p (r b j)"),
                                  out_sq[:, :, :, :].rearrange("p r s d -> p (r s) d"), AX.X, ALU.add)\
                    .then_inc(S["out_ms"].sem, 1)

            def OY(c):
                dve.wait_ge(*S["out_f"](c, 1))
                dve.wait_ge(*S["yg"](c, 0))
                for r in range(2):
                    last = dve.tensor_tensor(y[:, :, :, :].rearrange("p b (j r) d -> p b j r d", r=2)[:, :, :, r, :],
                                             work[1][:, r, :].rearrange("p (b j d) -> p b j d", b=BATCH, j=2),
                                             bcast(out_f[:, r, :, :], HD), ALU.mult)
                last.then_inc(S["y"].sem, 1)

            def MU(c, g):
                bank = (GRAM0, GRAM1, 0)[g]
                dve.wait_ge(*S["dw_ps"](c, g + 1))
                dve.wait_ge(*S["decayed"](c + 1, 0))
                dve.tensor_tensor(M[:, g, :, :], BANK[bank].rearrange("p (s d) -> p s d", d=HD), decayed[:, g, :, :], ALU.add)\
                    .then_inc(S["mom"].sem, 1)

            def SS(bank, c, g):
                ps = BANK[bank[0]]
                dve.wait_ge(*S["ss_ps"](c, g + 1))
                dve.tensor_copy(ss[:, g, :], ps[:, 0:8]).then_inc(S["ss"].sem, 1)

            def MR(c, g):
                dve.wait_ge(*S["mom_sq"](c, g + 1))
                dve.tensor_reduce(m_ss[:, g, :], m_sq[:, g, :, :], AX.X, ALU.add).then_inc(S["mom_ss"].sem, 1)

            def SN(c, g):
                dve.wait_ge(*S["fro"](c, g + 1))
                dve.tensor_scalar(fro_e[:, g, :], fro[:, g, :], GRAD_GAIN * 1e-7, None, ALU.add).then_inc(S["fro_eps"].sem, 1)
                dve.wait_ge(*S["fro_eps"](c, g + 1))
                dve.reciprocal(rfro[:, g, :], fro_e[:, g, :]).then_inc(S["rfro"].sem, 1)
                dve.wait_ge(*S["rfro"](c, g + 1))
                dve.wait_ge(*S["x_ps"](c, 0))
                dve.tensor_tensor(X[:, g, :, :], M[:, g, :, :], bcast(rfro[:, g, :], HD), ALU.mult).then_inc(S["x0"].sem, 1)

            def NB(bank, c, it, g):
                ps = BANK[bank[0]].rearrange("p (s d) -> p s d", d=HD)
                dve.wait_ge(*S["b_ps"](c, 3 * it + g + 1))
                if it:
                    dve.wait_ge(*S["x_ps"](c, 3 * (it - 1) + g + 1))
                stt(B[:, g, :, :], ps, NS_F[it], A[:, g, :, :], ALU.mult, ALU.add).then_inc(S["B"].sem, 1)

            def NX(bank, c, it, g):
                ps = BANK[bank[0]].rearrange("p (s d) -> p s d", d=HD)
                dve.wait_ge(*S["x_ps"](c, 3 * it + g + 1))
                if it < NIT - 1:
                    stt(X[:, g, :, :], ps, NS_E[it], X[:, g, :, :], ALU.mult, ALU.add).then_inc(S["X"].sem, 1)
                else:
                    dve.wait_ge(*S["V"](c, g + 1))
                    stt(U[:, g, :, :], ps, NS_E[it] * NS_S, V[:, g, :, :], ALU.mult, ALU.add).then_inc(S["X"].sem, 1)

            def NV(c, g):
                dve.wait_ge(*S["X"](c, 3 * (NIT - 2) + g + 1))
                stt(V[:, g, :, :], X[:, g, :, :], NS_S, W[:, g, :, :], ALU.mult, ALU.add).then_inc(S["V"].sem, 1)

            def RN(c, g):
                dve.wait_ge(*S["u_sq"](c, g + 1))
                dve.tensor_reduce(u_ss[:, g, :], u_sq[:, g, :, :], AX.X, ALU.add).then_inc(S["u_ss"].sem, 1)
                dve.wait_ge(*S["u_n"](c, g + 1))
                dve.tensor_scalar(u_e[:, g, :], u_n[:, g, :], 1e-5, None, ALU.add).then_inc(S["u_eps"].sem, 1)
                dve.wait_ge(*S["u_eps"](c, g + 1))
                dve.reciprocal(u_r[:, g, :], u_e[:, g, :]).then_inc(S["u_r"].sem, 1)
                dve.wait_ge(*S["u_r"](c, g + 1))
                dve.tensor_tensor(u_f[:, g, :], u_r[:, g, :], row_norm[:, g, :], ALU.mult).then_inc(S["u_f"].sem, 1)
                dve.wait_ge(*S["u_f"](c, g + 1))
                dve.tensor_tensor(W[:, g, :, :], U[:, g, :, :], bcast(u_f[:, g, :], HD), ALU.mult).then_inc(S["W"].sem, 1)

            def SC(bank, c, b):
                ps = BANK[bank[0]]
                wait_apart(dve, S["s_ps"](c, b + 1), S["pt_ps"](c, max(b - 1, 0)), S["m_prev"](c, 0))
                for hd in range(NAH):
                    last = dve.tensor_tensor_reduce(masked[:, b % 2, hd, :], ps[:, hd * 256:(hd + 1) * 256], mask[:, :], 1.0,
                                                    -3.0e38, ALU.add, ALU.max, smax[:, b, hd:hd + 1])
                last.then_inc(S["masked"].sem, 1)
                dve.wait_ge(*S["masked"](c, b + 1))
                dve.tensor_scalar(nmax[:, b, :], smax[:, b, :], -SCALE, None, ALU.mult).then_inc(S["neg_max"].sem, 1)

            def PT(c, b):
                dve.wait_ge(*S["prob"](c, b + 1))
                dve.wait_ge(*S["comb"](c, 0))
                dve.reciprocal(rsums[:, b, :], psums[:, b, :]).then_inc(S["psum_r"].sem, 1)

            def PV(bank, c, b):
                ps = BANK[bank[0]]
                dve.wait_ge(*S["pv_ps"](c, b + 1))
                dve.wait_ge(*S["yg"](c, 1))
                dve.wait_ge(*S["psum_r"](c, b + 1))
                dve.wait_ge(*S["ct_ps"](c, 0))
                for hd in range(NAH):
                    last = stt(comb[:, b, hd * P:(hd + 1) * P], ps[:, hd * P:(hd + 1) * P], rsums[:, b, hd:hd + 1],
                               yg[:, b, 2 * hd:2 * hd + 2, :].rearrange("p h d -> p (h d)"), ALU.mult, ALU.add)
                last.then_inc(S["comb"].sem, 1)

            wo_ps = {}

            def WO(bank, c, b):
                wo_ps[b] = ps = BANK[bank[0]]
                dve.wait_ge(*S["wo_ps"](c, b + 1))
                dve.bn_stats(st2[:, b, :], ps[:, 0:DIM]).then_inc(S["wo_st"].sem, 1)
                wait_apart(dve, S["wo_st"](c, b + 1))
                dve.bn_aggr(mv2[:, b, :], st2[:, b, :]).then_inc(S["wo_mv"].sem, 1)

            def WON(c, b):
                dve.wait_ge(*S["wo_rstd"](c, b + 1))
                if b == 0:
                    dve.wait_ge(*S["stored"](c, 0))
                dve.tensor_scalar(wo_n[:, b, :], wo_ps[b][:, 0:DIM], mv2[:, b, 0:1], rstd2[:, b:b + 1], ALU.subtract, ALU.mult)\
                    .then_inc(S["wo_n"].sem, 1)

            def L2(c, b):
                dve.wait_ge(*S["x1"](c, b + 1))
                dve.bn_stats(st3[:, b, :], x1[:, b, :]).then_inc(S["l2_st"].sem, 1)
                wait_apart(dve, S["l2_st"](c, b + 1))
                dve.bn_aggr(mv3[:, b, :], st3[:, b, :]).then_inc(S["l2_mv"].sem, 1)

            def L2N(c, b):
                dve.wait_ge(*S["l2_rstd"](c, b + 1))
                dve.wait_ge(*S["nt_ps"](c, 0))
                dve.tensor_scalar(xn2[:, b, :], x1[:, b, :], mv3[:, b, 0:1], rstd3[:, b:b + 1], ALU.subtract, ALU.mult)\
                    .then_inc(S["xn2"].sem, 1)

            def F2(bank, c, b):
                ps = BANK[bank[0]]
                dve.wait_ge(*S["f2_ps"](c, b + 1))
                dve.tensor_tensor(f2[:, b, :], ps[:, 0:DIM], b2[:, :], ALU.add).then_inc(S["f2"].sem, 1)
                dve.wait_ge(*S["f2"](c, b + 1))
                dve.bn_stats(st4[:, b, :], f2[:, b, :]).then_inc(S["f2_st"].sem, 1)
                wait_apart(dve, S["f2_st"](c, b + 1))
                dve.bn_aggr(mv4[:, b, :], st4[:, b, :]).then_inc(S["f2_mv"].sem, 1)

            def F2N(c, b):
                dve.wait_ge(*S["f2_rstd"](c, b + 1))
                dve.wait_ge(*S["outb"](c, 0))
                dve.tensor_scalar(f2_n[:, b, :], f2[:, b, :], mv4[:, b, 0:1], rstd4[:, b:b + 1], ALU.subtract, ALU.mult)\
                    .then_inc(S["f2_n"].sem, 1)

            def MUR(c, g):
                MU(c, g)
                MR(c, g)

            of_next = {"LN1": LN1, "SM": SM, "SP": SP, "MS": MS, "MM": MM, "VV": VV, "SI": SI, "NQ": NQ, "TR": TR}
            of_this = {"EL": EL, "ELB": ELB, "FE": FE, "OE": OE, "OY": OY, "MU": MUR, "SS": SS, "SN": SN, "NB": NB, "NX": NX,
                       "NV": NV, "RN": RN, "S": SC, "PT": PT, "PV": PV, "WO": WO, "WON": WON, "L2": L2, "L2N": L2N, "F2": F2,
                       "F2N": F2N}
            READS = ("SM", "MM", "VV", "TR", "SS", "NB", "NX", "S", "PV", "WO", "F2")

            def run(steps, c):
                plan = bank_plan(steps)
                for step in steps:
                    kind, *arg = step
                    bank = [plan[step]] if kind in READS else []
                    if kind in of_next:
                        of_next[kind](*bank, c + 1, *arg)
                    elif kind in of_this:
                        of_this[kind](*bank, c, *arg)

            dve.wait_ge(ld_w, 96)
            for g in range(3):
                dve.tensor_copy(W[:, g, :, :].rearrange("p (b j) d -> p b (j d)", j=2),
                                w_in[:, g, :, :].rearrange("p j d -> p (j d)").unsqueeze(1).to_broadcast([P, BATCH, 2 * HD]))\
                    .then_inc(S["W"].sem, 1)
            dve.wait_ge(w_sq0, 1)
            dve.tensor_reduce(u_ss[:, :, :].rearrange("p g s -> p (g s)"), u_sq[:, :, :, :].rearrange("p g s d -> p (g s) d"),
                              AX.X, ALU.add).then_inc(w_ss0, 1)
            dve.wait_ge(ld_misc, MISC)
            dve.tensor_scalar(g_half[:, :], g_raw[:, :], 0.5, None, ALU.mult).then_inc(folded, 1)
            dve.wait_ge(consts, 1)
            run(FIRST, -1)
            dve.wait_ge(folded, 1)
            with dve.Fori(0, CHUNKS - 1) as c:
                run(BODY, c)
            run(LAST, CHUNKS - 1)

        @block.gpsimd
        def _(pool):
            def tt(out_, in0, in1, op=ALU.mult):
                return pool.tensor_tensor(out_, in0, in1, op)

            def rsqrt(c, n, mv, var, rstd, ready, mid, done, sl):
                wait_apart(pool, S[ready](c, n))
                pool.tensor_scalar(var[:, sl], mv[:, sl, 1], LN_EPS, None, ALU.add).then_inc(S[mid].sem, 1)
                pool.wait_ge(*S[mid](c, n))
                k = sl.stop - sl.start
                tt(rstd[:, sl], var[:, sl], neg_half[:, 0:k], ALU.pow).then_inc(S[done].sem, 1)

            def LN1(c):
                rsqrt(c, 1, mv1, var1, rstd1, "ln1_mv", "ln1_var", "ln1_rstd", slice(0, BATCH))
                if isinstance(c, int) and c == 0:
                    pool.tensor_copy(x_res[:, :, :], x_in[:, :, :]).then_inc(S["x_res"].sem, 1)

            def MP(c):
                pool.wait_ge(*S["mm"](c, 1))
                pool.wait_ge(*S["mom"](c, 0))
                pool.wait_ge(*S["X"](c, 0))
                for g in range(3):
                    tt(decayed[:, g, :, :], M[:, g, :, :], bcast(mm[:, :], HD)).then_inc(S["decayed"].sem, 1)

            def SI(c, b):
                pool.wait_ge(*S["silu"](c, b + 1))
                if b >= 2:
                    pool.wait_ge(*S["ssq"](c, b - 1))
                tt(sq[:, b % 2, :], silu[:, b, 0:512], silu[:, b, 0:512]).then_inc(S["sq"].sem, 1)

            def NQ(c, b):
                pool.wait_ge(*S["ssq"](c, b + 1))
                tt(nq[:, b, :], ssq[:, b, :], half[:, 0:8], ALU.pow).then_inc(S["nq"].sem, 1)
                pool.wait_ge(*S["rq"](c, b + 1))
                tt(qn[:, b, 0:512].rearrange("p (h d) -> p h d", d=HD), silu[:, b, 0:512].rearrange("p (h d) -> p h d", d=HD),
                   bcast(rq[:, b, :], HD)).then_inc(S["qn"].sem, 1)
                pool.wait_ge(*S["qn"](c, b + 1))
                pool.wait_ge(*S["lr"](c, 1))
                pool.wait_ge(*S["dw_ps"](c, 0))
                rates = lr[:, b, :].rearrange("p (h i) -> p h i", i=3)
                kk = qn[:, b, 256:512].rearrange("p (h d) -> p h d", d=HD)
                tt(kl0[:, b, :, :], kk, bcast(rates[:, :, 0], HD))
                tt(kl2[:, b, :, :], kk, bcast(rates[:, :, 2], HD))
                tt(vl1[:, b, :, :].rearrange("p (j r) d -> p j r d", j=2),
                   silu[:, b, 512:768].rearrange("p (j r d) -> p j r d", j=2, r=2),
                   bcast(rates[:, :, 1].rearrange("p (r j) -> p j r", j=2), HD))\
                    .then_inc(S["klv"].sem, 1)

            def EL(c, bp):
                wait_apart(pool, S["gba_tanh"](c, bp + 1), S["dsig"](c, 0))
                pool.tensor_scalar(one_t[:, bp, :, :], gba_t[:, bp, :, :], 1.0, None, ALU.add).then_inc(S["one_t"].sem, 1)
                pool.wait_ge(*S["sg"](c, bp + 1))
                pool.wait_ge(*S["dh"](c, 1))
                tt(dhbm[:, bp, :, :], dh[:, bp, :, :, :, :].rearrange("p r y j d -> p (r y j) d"), sg[:, bp, :, :])\
                    .then_inc(S["dhbm"].sem, 1)

            def OE(c):
                wait_apart(pool, S["out_ms"](c, 1))
                pool.tensor_scalar(out_v[:, :, :, :], out_ms[:, :, :, :], 1.0 / HD, 4 * 1e-5, ALU.mult, ALU.add)\
                    .then_inc(S["out_var"].sem, 1)
                pool.wait_ge(*S["out_var"](c, 1))
                tt(out_rs[:, :, :, :].rearrange("p r b j -> p (r b j)"), out_v[:, :, :, :].rearrange("p r b j -> p (r b j)"),
                   neg_half[:, 0:16], ALU.pow).then_inc(S["out_rs"].sem, 1)
                pool.wait_ge(*S["out_rs"](c, 1))
                tt(out_f[:, :, :, :], out_rs[:, :, :, :], ms[:, :, 4:8].rearrange("p b (j r) -> p r b j", r=2))\
                    .then_inc(S["out_f"].sem, 1)

            def OY(c):
                pool.wait_ge(*S["y"](c, 1))
                pool.wait_ge(*S["comb"](c, 0))
                tt(yg[:, :, :, :].rearrange("p b h d -> p (b h) d"), y[:, :, :, :].rearrange("p b h d -> p (b h) d"),
                   g_half[:, :].unsqueeze(1).to_broadcast([P, 16, HD])).then_inc(S["yg"].sem, 1)

            def SS(c, g):
                pool.wait_ge(*S["ss"](c, g + 1))
                tt(fro[:, g, :], ss[:, g, :], half[:, 0:8], ALU.pow).then_inc(S["fro"].sem, 1)

            def RN(c, g):
                pool.wait_ge(*S["u_ss"](c, g + 1))
                tt(u_n[:, g, :], u_ss[:, g, :], half[:, 0:8], ALU.pow).then_inc(S["u_n"].sem, 1)

            def PRV(c):
                wait_apart(pool, S["s_ps"](c, 4))
                pool.tensor_copy(akT[:, :, :, 0, :].rearrange("p h b t -> p (h b) t"),
                                 akT[:, :, :, 1, :].rearrange("p h b t -> p (h b) t")).then_inc(S["k_prev"].sem, 1)
                wait_apart(pool, S["pv_ps"](c, 4))
                pool.tensor_copy(v_prev[:, :, :], raw[:, :, 512:768]).then_inc(S["v_prev"].sem, 1)
                wait_apart(pool, S["masked"](c, 4))
                pool.tensor_copy(mask[:, 0:P], mask_prev[:, :]).then_inc(S["m_prev"].sem, 1)

            def WO(c, b):
                rsqrt(c, b + 1, mv2, var2, rstd2, "wo_mv", "wo_var", "wo_rstd", slice(b, b + 1))

            def WON(c, b):
                pool.wait_ge(*S["wo_n"](c, b + 1))
                if b == 0:
                    pool.wait_ge(*S["outb"](c, 0))
                    pool.wait_ge(*S["x_res"](c + 1, 0))
                tt(x1[:, b, :], wo_n[:, b, :], x_res[:, b, :], ALU.add).then_inc(S["x1"].sem, 1)

            def XRES(c):
                wait_apart(pool, S["x1"](c, 4), S["x_in"](c + 1, 16))
                pool.tensor_copy(x_res[:, :, :], x_in[:, :, :]).then_inc(S["x_res"].sem, 1)

            def L2(c, b):
                rsqrt(c, b + 1, mv3, var3, rstd3, "l2_mv", "l2_var", "l2_rstd", slice(b, b + 1))

            def F2(c, b):
                rsqrt(c, b + 1, mv4, var4, rstd4, "f2_mv", "f2_var", "f2_rstd", slice(b, b + 1))

            def F2N(c, b):
                pool.wait_ge(*S["f2_n"](c, b + 1))
                tt(outb[:, b, :], f2_n[:, b, :], x1[:, b, :], ALU.add).then_inc(S["outb"].sem, 1)

            of_next = {"LN1": LN1, "MP": MP, "SI": SI, "NQ": NQ}
            of_this = {"EL": EL, "OE": OE, "OY": OY, "SS": SS, "RN": RN, "PRV": PRV, "WO": WO, "WON": WON, "XRES": XRES,
                       "L2": L2, "F2": F2, "F2N": F2N}

            def run(steps, c):
                for kind, *arg in steps:
                    if kind in of_next:
                        of_next[kind](c + 1, *arg)
                    elif kind in of_this:
                        of_this[kind](c, *arg)

            for t, v in ((ident, 0.0), (ones_blk, 0.0), (ones_avg, 0.5 / CHUNK), (half, 0.5), (neg_half, -0.5),
                         (mask_prev, 0.0), (mask, 0.0)):
                last = pool.memset(t[:, :], v)
            pool.memset(small_bias[:, 0:12], BASE_LR_INV)
            pool.memset(v_prev[:, :, :], 0.0)
            pool.memset(akT[:, :, :, 0, :], 0.0)
            pool.memset(M[:, :, :, :], 0.0).then_inc(zeroed, 1)
            pool.wait_ge(zeroed, 1)
            pool.affine_select(out=ident[:, :], in_=ident[:, :], compare_op=ALU.not_equal, fill=1.0, base=0,
                               pattern=[[-1, P]], channel_multiplier=1)
            pool.affine_select(out=mask_prev[:, :], in_=mask_prev[:, :], compare_op=ALU.is_ge, fill=NEG, base=0,
                               pattern=[[1, P]], channel_multiplier=-1)
            pool.affine_select(out=mask[:, P:2 * P], in_=mask[:, P:2 * P], compare_op=ALU.is_ge, fill=NEG, base=0,
                               pattern=[[-1, P]], channel_multiplier=1)
            pool.memset(mask[:, 0:P], NEG)
            pool.memset(ones_blk[0:64, 0:64], 1.0).then_inc(zeroed, 1)
            pool.wait_ge(zeroed, 2)
            pool.memset(ones_blk[64:128, 64:128], 1.0).then_inc(consts, 1)
            pool.wait_ge(w_ss0, 1)
            pool.wait_ge(consts, 1)
            tt(row_norm[:, :, :].rearrange("p g s -> p (g s)"), u_ss[:, :, :].rearrange("p g s -> p (g s)"), half[:, 0:24], ALU.pow)\
                .then_inc(norms, 1)
            pool.wait_ge(norms, 1)
            run(FIRST, -1)
            pool.wait_ge(folded, 1)
            with pool.Fori(0, CHUNKS - 1) as c:
                run(BODY, c)
            run(LAST, CHUNKS - 1)


_INS = ['L0_attn_x', 'L0_attn_Wqkv', 'L0_attn_Wlr', 'L0_attn_Wm', 'L0_attn_bm', 'L0_attn_Ws', 'L0_attn_bs', 'L0_attn_Wo',
        'L0_attn_w0', 'L0_attn_w1', 'L0_attn_w2', 'L0_attn_o_norm_g', 'L0_attn_qk_scale', 'L0_attn_qk_offset',
        'L0_ffn_proj1', 'L0_ffn_proj1_bias', 'L0_ffn_proj2', 'L0_ffn_proj2_bias']


def kernel(**inputs):
    import concourse.bacc as _bacc
    from concourse.bass_utils import run_bass_kernel_spmd as _run

    nc = _bacc.Bacc("TRN2", target_bir_lowering=False, num_devices=1)
    arrays, args = {}, []
    for name in _INS:
        a = np.ascontiguousarray(inputs[name])
        arrays[f"in_{name}_dram"] = a
        args.append(nc.dram_tensor(f"in_{name}_dram", a.shape, mybir.dt.from_np(a.dtype), kind="ExternalInput").ap())
    args.append(nc.dram_tensor("out_0_dram", (BATCH, SEQ, DIM), F32, kind="ExternalOutput").ap())
    layer_kernel(nc, *args)
    r = _run(nc, [arrays], core_ids=[0])
    return r.results[0]["out_0_dram"]
```

```python
from contextlib import ExitStack

import numpy as np

import concourse.bass as bass
from concourse import mybir

F32 = mybir.dt.float32
ALU = mybir.AluOpType
ACT = mybir.ActivationFunctionType
AX = mybir.AxisListType

P = 128
BATCH, SEQ, DIM = 4, 512, 256
CHUNK = 128
CHUNKS = SEQ // CHUNK
HD = 64
NH = DIM // HD
KC = DIM // P
HID = 1024
HC = HID // P
NAH = 2
SMALL = 5 * NH
LN_EPS = 1e-5
BASE_LR = 0.01
BASE_LR_INV = float(BASE_LR + np.log(-np.expm1(-BASE_LR)))
SCALE = float(P) ** -0.5
NEG = -1.0e30
NS = [(4.0848, -6.8946, 2.927), (3.9505, -6.3029, 2.6377), (3.7418, -5.5913, 2.3037),
      (2.8769, -3.1427, 1.2046), (2.8366, -3.0525, 1.2012)]
NIT = len(NS)
GRAD_GAIN = 4.0

NS_F, NS_E, NS_S = [], [], 1.0
for _a, _b, _c in NS:
    NS_F.append(_c * NS_S * NS_S / _b)
    NS_E.append(_b * NS_S * NS_S / _a)
    NS_S *= _a

G_W1, G_W2, G_W0 = 0, 1, 2


class Signal:

    def __init__(self, sem, per_chunk, ahead):
        self.sem, self.per_chunk, self.ahead = sem, per_chunk, ahead

    def __call__(self, c, n):
        return self.sem, c * self.per_chunk + (n + self.ahead)


RAISED_AHEAD = dict(
    tensor=("ct_ps", "dh_ps", "dw_ps", "f2_ps", "fw_ps", "gba_ps", "mm_ps", "nt_ps", "out_ps", "pt_ps", "s_ps", "tr_ps", "v_ps",
            "xT_ps", "x_ps"),
    scalar=("A", "W1D", "WT", "XT", "att_T", "cT", "dh", "h", "lr_log", "one_t", "pT", "qk_raw", "xn2T", "xnT"),
    vector=("B", "X", "comb", "dgba", "dsig", "el", "f2", "fw_silu", "gT", "lr", "masked", "mm", "mom", "ms", "psum_r", "silu",
            "ss", "ssq", "ttt_T", "v_raw", "wo_n", "yg"),
    gpsimd=("decayed", "dhbm", "k_prev", "klv", "m_prev", "out_f", "outb", "v_prev"),
    sync=("stored",),
)


RISES = dict(
    ln1_stats=1, ln1_mv=1, ln1_var=1, ln1_rstd=1, xn=1, xT_ps=2, xnT=2, 
    lr_neg=1, lr_exp=1, lr_log=1, lr=1, ms_tanh=1, ms=1, mm_ps=1, mm=1, decayed=3,
    qk_ps=4, qk_raw=4, v_ps=4, v_raw=4, sig=4, silu=4, sq=4, ssq=4, nq=4, nq_eps=4, rq=4, qn=4, klv=4,
    tr_ps=10, att_T=4, ttt_T=6,
    gba_ps=2, gba_tanh=2, dh_ps=1, dh=1, sg=2, el=2, one_t=2, dhbm=2, dsig=2, dgba=2, dw_ps=3,
    fw_ps=2, fw_tanh=2, fw_silu=2, gT=2, out_ps=2, out_sq=1, out_ms=1, out_var=1, out_rs=1, out_f=1, y=1, yg=1,
    mom=3, mom_sq=3, mom_ss=3, ss_ps=3, ss=3, fro=3, fro_eps=3, rfro=3, x0=3,
    xt_ps=15, XT=15, a_ps=15, A=15, b_ps=15, B=15, x_ps=15, X=15, V=3,
    u_sq=3, u_ss=3, u_n=3, u_eps=3, u_r=3, u_f=3, W=3, w_ps=3, WT=3, W1D=1,
    s_ps=4, masked=4, neg_max=4, prob=4, psum_r=4, pt_ps=4, pT=4, pv_ps=4, comb=4, ct_ps=4, cT=4,
    k_prev=1, v_prev=1, m_prev=1,
    wo_ps=4, wo_st=4, wo_mv=4, wo_var=4, wo_rstd=4, wo_n=4, x1=4,
    l2_st=4, l2_mv=4, l2_var=4, l2_rstd=4, xn2=4, nt_ps=4, xn2T=4, f1_ps=8, h=8,
    f2_ps=4, f2=4, f2_st=4, f2_mv=4, f2_var=4, f2_rstd=4, f2_n=4, outb=4,
    w_sq=1, w_ss=1, w_norm=1, mt_ps=8, mlp_T=8,
    x_in=16, x_again=16, stored=64,
)



def steps(text):
    return [(word.split(".")[0], *map(int, word.split(".")[1:])) for word in text.split()]


FIRST = steps("""
    XT LN1 QK.0 LNX ZS VV.0 SI.0 MT.0 WI QK.1 VV.1 NQ.0 QK.2 SI.1 VV.2 QK.3 SI.2 VV.3 SM NQ.1 SP NQ.2 NR.0 WX.0 SI.3
    TR.0 TR.1 NR.1 NQ.3 TR.2 MS TR.3 NR.2 NR.3 KL.0 TR.4 KL.1 KL.2 MT.1 MT.2 WX.1 TR.5 TR.6 KL.3 MM MT.3 TR.7 MT.4
    MT.5 MT.6 TR.8 MT.7 TR.9 WX.2 WN MP
""")
BODY = steps("""
    GB.0 LN1 FE.0 FW.0 EL.0 DH GB.1 LNX FW.1 S.0 XT FE.1 ELB.0 EL.1 DW.0 S.1 ELB.1 OUT.0 OUT.1 DW.1 OE MU.0 MU.1 S.2
    PT.0 PT.1 MR.0 MU.2 SS.0 MR.1 OY SN.0 PV.0 PT.2 MR.2 SS.1 S.3 SS.2 SN.1 SN.2 TX.0.0 PV.1 NA.0.0 TX.0.1 PT.3 PV.2
    NB.0.0 TX.0.2 CT.0 NA.0.1 NX.0.0 CT.1 WO.0 NB.0.1 WO.1 CT.2 TX.1.0 WON.0 PV.3 NX.0.1 NA.0.2 WON.1 WO.2 NB.0.2 CT.3
    L2.0 WON.2 L2.1 NA.1.0 L2N.0 WO.3 TX.1.1 L2N.1 NT.0 PRV WON.3 NX.0.2 L2.2 NT.1 NB.1.0 QK.0 NA.1.1 TX.1.2 L2N.2
    L2.3 NX.1.0 VV.0 L2N.3 NB.1.1 NA.1.2 SI.0 TX.2.0 QK.1 NT.2 NQ.0 NX.1.1 NB.1.2 NR.0 NA.2.0 VV.1 SI.1 TX.2.1 NT.3
    NX.1.2 F1.0 NA.2.1 NB.2.0 F1.1 TX.2.2 NQ.1 NX.2.0 NB.2.1 NA.2.2 TX.3.0 NX.2.1 QK.2 NB.2.2 NR.1 NA.3.0 TX.3.1
    NX.2.2 NB.3.0 NA.3.1 TX.3.2 F1.2 VV.2 SI.2 NX.3.0 NV.0 NB.3.1 NQ.2 NA.3.2 F1.3 TX.4.0 NX.3.1 NR.2 NV.1 NB.3.2
    NA.4.0 TX.4.1 NX.3.2 NV.2 F1.4 NB.4.0 QK.3 VV.3 SI.3 NA.4.1 TX.4.2 KL.0 NX.4.0 TR.0 NB.4.1 KL.1 SM NA.4.2 F1.5 SP
    F1.6 NX.4.1 F1.7 NQ.3 RN.0 MS TR.1 NB.4.2 NR.3 TR.3 TR.2 KL.2 RN.1 F2.0 NX.4.2 TR.5 RM.0 TR.4 RN.2 RM.1 F2N.0 TR.6
    F2.1 F2.2 MM TR.7 WX.0 KL.3 TR.9 RM.2 WX.1 TR.8 F2.3 WX.2 F2N.1 F2N.2 MP F2N.3
""")
LAST = steps("""
    FE.0 FW.0 S.0 FW.1 S.1 OUT.0 FE.1 OUT.1 PT.0 OE S.2 PT.1 OY PV.0 PT.2 S.3 PV.1 CT.0 PV.2 PT.3 WO.0 CT.1 PV.3 WON.0
    WO.1 CT.2 L2.0 WON.1 CT.3 WO.2 L2N.0 NT.0 L2.1 WON.2 L2N.1 WO.3 L2.2 NT.1 F1.0.0 F1.1.0 F1.2.0 F1.3.0 L2N.2 F1.4.0
    F1.5.0 F1.6.0 F1.7.0 NT.2 WON.3 L2.3 L2N.3 NT.3 F2.0 F1.0.1 F1.1.1 F1.2.1 F1.3.1 F1.4.1 F1.5.1 F1.6.1 F1.7.1 F2N.0
    F2.1 F2.2 F2N.1 F2N.2 F2.3 F2N.3
""")


WORK_BANKS = {"XT": 2, "MM": 1, "QK": 1, "VV": 1, "TR": 1, "S": 1, "PT": 1, "PV": 1, "CT": 1, "WO": 1, "NT": 1,
              "F1": 1, "F2": 1, "MT": 1}
UPDATE_BANKS = ("SS", "TX", "NB", "NX", "WX")
UPD0, UPD1, GRAM0, GRAM1 = 4, 5, 6, 7


def bank_plan(steps):
    plan, held, turn, upd_turn = {}, set(), 0, 0
    for step in steps:
        kind = step[0]
        if kind == "GB":
            held |= {2 * step[1], 2 * step[1] + 1}
        elif kind == "EL":
            held -= {2 * step[1], 2 * step[1] + 1}
        elif kind == "DW" and step[1] == 0:
            held |= {0}
        elif kind == "MU" and step[1] == G_W0:
            held -= {0}
        elif kind == "OUT" and step[1] == 0:
            held |= {2, 3}
        elif kind == "OE":
            held -= {2, 3}
        elif kind in WORK_BANKS:
            plan[step] = []
            for _ in range(WORK_BANKS[kind]):
                while turn % 4 in held:
                    turn += 1
                plan[step].append(turn % 4)
                turn += 1
        elif kind in UPDATE_BANKS:
            plan[step] = [UPD0 + upd_turn % 2]
            upd_turn += 1
    return plan


def layer_kernel(nc, x, Wqkv, Wlr, Wm, bm, Ws, bs, Wo, w0, w1, w2, o_norm_g, qk_scale, qk_offset,
                 proj1, proj1_bias, proj2, proj2_bias, out):
    with ExitStack() as ctx:
        def sb(name, *shape):
            return ctx.enter_context(nc.sbuf_tensor(name, [P, *shape], F32))

        def share(whole, at, *shape):
            flat = whole[tuple([slice(None)] * len(whole.shape))]
            names = "abcdef"[:len(whole.shape) - 1]
            if len(names) > 1:
                flat = flat.rearrange(f"p {' '.join(names)} -> p ({' '.join(names)})")
            flat = flat[:, at:at + int(np.prod(shape))]
            names = "abcdef"[:len(shape)]
            if len(names) == 1:
                return flat
            return flat.rearrange(f"p ({' '.join(names)}) -> p {' '.join(names)}", **dict(zip(names, shape)))

        def sem(name):
            return ctx.enter_context(nc.semaphore(name))

        gram = ctx.enter_context(nc.psum_tensor("gram", [P, 2, 512], F32))
        upd = [ctx.enter_context(nc.psum_tensor(f"upd{n}", [P, 512], F32)) for n in range(2)]
        work = [ctx.enter_context(nc.psum_tensor(f"work{n}", [P, 2, 512], F32)) for n in range(2)]
        BANK = [work[0][:, 0, :], work[0][:, 1, :], work[1][:, 0, :], work[1][:, 1, :], upd[0][:, :], upd[1][:, :],
                gram[:, 0, :], gram[:, 1, :]]

        ident = sb("ident", P)
        ones_blk = sb("ones_blk", P)
        ones_avg = sb("ones_avg", HD)
        mask = sb("mask", 2 * P)
        mask_prev = sb("mask_prev", P)
        half = sb("half", 32)
        neg_half = sb("neg_half", 32)
        wqkv = sb("wqkv", KC, 3 * DIM + SMALL)
        wsmall = wqkv[:, :, 3 * DIM:]
        small_bias = sb("small_bias", SMALL)
        wo = sb("wo", KC, DIM)
        p1T = sb("p1T", KC, HID)
        p2T = sb("p2T", HC, DIM)
        b1 = sb("b1", HC)
        b2 = sb("b2", DIM)
        g_raw = sb("g_raw", HD)
        g_half = sb("g_half", HD)
        qk_sc = sb("qk_sc", KC, 2)
        qk_of = sb("qk_of", KC, 2)
        row_ss = sb("row_ss", 3, 2)
        row_norm = sb("row_norm", 3, 2)
        x_in = sb("x_in", BATCH, DIM)
        st1 = sb("st1", BATCH, 6)
        mv1 = sb("mv1", BATCH, 2)
        var1 = sb("var1", BATCH)
        rstd1 = sb("rstd1", BATCH)
        xnT = sb("xnT", KC, BATCH * P)
        small = sb("small", BATCH, SMALL)
        lr_neg = sb("lr_neg", BATCH, 12)
        lr_exp = sb("lr_exp", BATCH, 12)
        lr_log = sb("lr_log", BATCH, 12)
        lr = sb("lr", BATCH, 12)
        ms_t = sb("ms_t", BATCH, 8)
        ms = sb("ms", BATCH, 8)
        mm = sb("mm", 8)
        decayed = sb("decayed", 3, 8, HD)
        raw = sb("raw", BATCH, 3 * DIM)
        silu = sb("silu", BATCH, 3 * DIM)
        ssq = sb("ssq", BATCH, 8)
        nq = sb("nq", BATCH, 8)
        nqe = sb("nqe", BATCH, 8)
        rq = sb("rq", BATCH, 8)
        kl0 = sb("kl0", BATCH, NH, HD)
        kl2 = sb("kl2", BATCH, NH, HD)
        vl1 = sb("vl1", BATCH, NH, HD)
        aqT = sb("aqT", NAH, BATCH, P)
        akT = sb("akT", NAH, BATCH, 2, P)
        tttT = sb("tttT", 3, 2, BATCH, P)
        W = sb("W", 3, BATCH * 2, HD)
        WT02 = sb("WT02", BATCH, 2, 2, 2, HD)
        W1T = sb("W1T", BATCH, 2, 2, HD)
        W1D = sb("W1D", BATCH, 2, 2, HD)
        out_ms = sb("out_ms", BATCH, NH)
        out_v = sb("out_v", BATCH, NH)
        out_rs = sb("out_rs", BATCH, NH)
        out_f = sb("out_f", BATCH, NH)
        y = sb("y", BATCH, NH, HD)
        M = sb("M", 3, 8, HD)
        m_ss = sb("m_ss", 3, 8)
        ss = sb("ss", 3, 8)
        fro = sb("fro", 3, 8)
        fro_e = sb("fro_e", 3, 8)
        rfro = sb("rfro", 3, 8)
        X = sb("X", 3, 8, HD)
        XT = sb("XT", 3, 8, HD)
        A = sb("A", 3, 8, HD)
        B = sb("B", 3, 8, HD)
        u_ss = sb("u_ss", 3, 8)
        u_n = sb("u_n", 3, 8)
        u_e = sb("u_e", 3, 8)
        u_r = sb("u_r", 3, 8)
        u_f = sb("u_f", 3, 8)
        masked = sb("masked", 2, 2, 2 * P)
        smax = sb("smax", BATCH, 2)
        nmax = sb("nmax", BATCH, 2)
        psums = sb("psums", BATCH, 2)
        rsums = sb("rsums", BATCH, 2)
        pT = sb("pT", 2, 2, 2, P)
        v_prev = sb("v_prev", BATCH, DIM)
        st2 = sb("st2", BATCH, 6)
        mv2 = sb("mv2", BATCH, 2)
        var2 = sb("var2", BATCH)
        rstd2 = sb("rstd2", BATCH)
        x1 = sb("x1", BATCH, DIM)
        st3 = sb("st3", BATCH, 6)
        mv3 = sb("mv3", BATCH, 2)
        var3 = sb("var3", BATCH)
        rstd3 = sb("rstd3", BATCH)
        xn2T = sb("xn2T", KC, BATCH * P)
        h = sb("h", HC, BATCH * P)
        st4 = sb("st4", BATCH, 6)
        mv4 = sb("mv4", BATCH, 2)
        var4 = sb("var4", BATCH)
        rstd4 = sb("rstd4", BATCH)

        p1_raw, p2_raw = share(h, 0, HC, DIM), share(h, HC * DIM, KC, HID)
        gba_t, one_t, dxh, gms = (share(h, n * 1024, 2, 8, HD) for n in range(4))
        dsig, dgba = gms, dxh
        w_in = share(X, 0, 3, 2, HD)
        sg, dhbm = share(X, 0, 2, 8, HD), share(XT, 512, 2, 8, HD)
        gT = share(pT, 0, 2, 4, P)
        hidden = (share(A, 1024, 8, HD), share(X, 1024, 8, HD))
        sq = share(y, 0, 2, 2 * DIM)
        cT = share(aqT, 0, 2, KC, P)
        dh = share(A, 0, 2, 2, 2, 2, HD)
        fw_t = share(B, 0, 2, 512)
        fw_s = fw_t
        out_sq = share(B, 0, 2, 8, HD)
        m_sq, u_sq, U, V = XT, B, A, decayed
        rows_a = sb("rows_a", BATCH, DIM)
        wo_n = f2 = f2_n = outb = rows_a
        rows_b = sb("rows_b", BATCH, DIM)
        xn = xn2 = comb = rows_b
        prob = masked
        qn = silu

        raised_ahead = {name for names in RAISED_AHEAD.values() for name in names}
        S = {name: Signal(sem("s_" + name), n, int(name in raised_ahead)) for name, n in RISES.items()}
        ld_qkv, ld_small, ld_misc, ld_w, ld_p1, ld_p2, ld_wo = (sem(n) for n in (
            "ld_qkv", "ld_small", "ld_misc", "ld_w", "ld_p1", "ld_p2", "ld_wo"))
        zeroed = sem("zeroed")
        state_zeroed = sem("state_zeroed")
        consts = sem("consts")
        folded = sem("folded")
        MISC = 16 * 7

        def wait_apart(eng, *waits):
            waits = [(sem_, n if isinstance(n, int) else eng.to_reg(n)) for sem_, n in filter(None, waits)]
            eng.wait_ge(consts, 1)
            for sem_, n in waits:
                eng.wait_ge(sem_, n)

        def bcast(ap, n):
            return ap.unsqueeze(len(ap.shape)).to_broadcast([*ap.shape, n])

        def rows(c):
            return x[:, bass.ts(c, CHUNK), :].rearrange("b p d -> p b d")

        block = ctx.enter_context(nc.Block())

        @block.sync
        def _(sp):
            for name in RAISED_AHEAD["sync"]:
                sp.sem_inc(S[name].sem)
            sp.dma_start(x_in[:, :, :], rows(0)).then_inc(S["x_in"].sem, 16)
            sp.dma_start(wqkv[:, :, 0:3 * DIM], Wqkv.rearrange("(k p) n -> p k n", p=P)).then_inc(ld_qkv, 16)
            sp.dma_start(wsmall[:, :, 0:12], Wlr.rearrange("(k p) n -> p k n", p=P)).then_inc(ld_small, 16)
            sp.dma_start(wsmall[:, :, 12:16], Wm.rearrange("(k p) n -> p k n", p=P)).then_inc(ld_small, 16)
            sp.dma_start(wsmall[:, :, 16:20], Ws.rearrange("(k p) n -> p k n", p=P)).then_inc(ld_small, 16)
            sp.dma_start(small_bias[:, 12:16], bm.partition_broadcast(P)).then_inc(ld_misc, 16)
            sp.dma_start(small_bias[:, 16:20], bs.partition_broadcast(P)).then_inc(ld_misc, 16)
            sp.dma_start(g_raw[:, :], o_norm_g.partition_broadcast(P)).then_inc(ld_misc, 16)
            sp.dma_start(b2[:, :], proj2_bias.partition_broadcast(P)).then_inc(ld_misc, 16)
            sp.dma_start(qk_sc[:, :, :], qk_scale.rearrange("(k p) n -> p k n", p=P)).then_inc(ld_misc, 16)
            sp.dma_start(qk_of[:, :, :], qk_offset.rearrange("(k p) n -> p k n", p=P)).then_inc(ld_misc, 16)
            sp.dma_start(b1[:, :], proj1_bias.rearrange("(k p) -> p k", p=P), allow_slow_non_contiguous=True).then_inc(ld_misc, 16)
            sp.wait_ge(ld_qkv, 16)
            for n, w in enumerate((w1, w2, w0)):
                for i in range(2):
                    sp.dma_start(w_in[64 * i:64 * i + 64, n, :, :], w[2 * i:2 * i + 2, :, :].rearrange("j r d -> r j d"))\
                        .then_inc(ld_w, 16)
            sp.dma_start(p1_raw[:, :, :], proj1.rearrange("(n p) e -> p n e", p=P)).then_inc(ld_p1, 16)
            sp.dma_start(p2_raw[:, :, :], proj2.rearrange("(k p) n -> p k n", p=P)).then_inc(ld_p2, 16)
            sp.dma_start(wo[:, :, :], Wo.rearrange("(k p) n -> p k n", p=P)).then_inc(ld_wo, 16)
            sp.dma_start(x1[:, :, :], rows(0)).then_inc(S["x_again"].sem, 16)

            def stores(c):
                for b in range(BATCH):
                    sp.wait_ge(*S["outb"](c, b + 1))
                    sp.dma_start(out[b, bass.ts(c, CHUNK), :], outb[:, b, :]).then_inc(S["stored"].sem, 16)

            def rows_in(c):
                sp.wait_ge(*S["xn"](c - 1, 1))
                sp.dma_start(x_in[:, :, :], rows(c)).then_inc(S["x_in"].sem, 16)

            def rows_again(c):
                sp.dma_start(x1[:, :, :], rows(c)).then_inc(S["x_again"].sem, 16)

            rows_in(1)
            with sp.Fori(0, CHUNKS - 2) as c:
                rows_in(c + 2)
                stores(c)
                rows_again(c + 1)
            stores(CHUNKS - 2)
            rows_again(CHUNKS - 1)
            stores(CHUNKS - 1)
            sp.wait_ge(*S["stored"](CHUNKS, 0))

        @block.tensor
        def _(pe):
            for name in RAISED_AHEAD["tensor"]:
                pe.sem_inc(S[name].sem)
            owner = {}

            def free(bank, signal, c, n, covered_by=()):
                last = owner.get(bank)
                owner[bank] = (signal, c, n)
                return None if last is None or last[0] in covered_by else S[last[0]](*last[1:])

            def take(bank, signal, c, n, covered_by=()):
                last = free(bank, signal, c, n, covered_by)
                if last is not None:
                    pe.wait_ge(*last)
                return BANK[bank]

            def all_read_out(c):
                for name in ("el", "dh", "mom", "gT", "yg", "masked", "pT", "comb", "cT", "wo_n", "xn2T", "h", "f2", "ss",
                             "XT", "A", "B", "X"):
                    pe.wait_ge(*S[name](c, 0))
                for name in ("xnT", "mm", "qk_raw", "v_raw", "att_T", "ttt_T", "WT", "W1D"):
                    pe.wait_ge(*S[name](c + 1, 0))
                owner.clear()

            def XT_(bank, c):
                pe.wait_ge(*S["xn"](c, 1))
                for k in range(KC):
                    ps = take(bank[k], "xnT", c, k + 1)
                    for b in range(BATCH):
                        mm_ = pe.transpose(ps[:, b * P:(b + 1) * P], xn[:, b, k * P:(k + 1) * P], ident[:, :])
                    mm_.then_inc(S["xT_ps"].sem, 1)

            def MM(bank, c):
                ps = BANK[bank[0]]
                wait_apart(pe, free(bank[0], "mm", c, 1), S["ms"](c, 1))
                for i in range(2):
                    mm_ = pe.matmul(ps[64 * i:64 * i + 64, 0:8], ones_avg[:, :],
                                    ms[:, :, 2 * i:2 * i + 2], start=True, stop=True)
                mm_.then_inc(S["mm_ps"].sem, 1)

            def QK(bank, c, b):
                pe.wait_ge(ld_qkv, 16)
                ps = take(bank[0], "qk_raw", c, b + 1)
                pe.wait_ge(*S["xnT"](c, 2))
                for k in range(KC):
                    mm_ = pe.matmul(ps, xnT[:, k, b * P:(b + 1) * P], wqkv[:, k, 0:512], start=(k == 0), stop=(k == KC - 1))
                mm_.then_inc(S["qk_ps"].sem, 1)

            def VV(bank, c, b):
                pe.wait_ge(ld_small, 48)
                ps = take(bank[0], "v_raw", c, b + 1)
                for k in range(KC):
                    mm_ = pe.matmul(ps[:, 0:DIM + SMALL], xnT[:, k, b * P:(b + 1) * P], wqkv[:, k, 512:],
                                    start=(k == 0), stop=(k == KC - 1))
                mm_.then_inc(S["v_ps"].sem, 1)

            def TR(bank, c, u):
                if u < 4:
                    ps = take(bank[0], "att_T", c, u + 1)
                    pe.wait_ge(*S["qk_raw"](c, 4))
                else:
                    ps = take(bank[0], "ttt_T", c, u - 3)
                    pe.wait_ge(*S["qn"](c, 4))
                for b in range(BATCH):
                    if u < 4:
                        src = raw[:, b, u * P:(u + 1) * P]
                    elif u < 8:
                        src = qn[:, b, (u - 4) * P:(u - 3) * P]
                    else:
                        src = silu[:, b, 512 + (u - 8) * P:512 + (u - 7) * P]
                    mm_ = pe.transpose(ps[:, b * P:(b + 1) * P], src, ident[:, :])
                mm_.then_inc(S["tr_ps"].sem, 1)

            def GB(c, bp):
                wait_apart(pe, free(2 * bp, "el", c, bp + 1), free(2 * bp + 1, "el", c, bp + 1))
                for y_ in range(2):
                    for j in range(2):
                        b = 2 * bp + y_
                        mm_ = pe.matmul(BANK[2 * bp + y_][:, j * 256:(j + 1) * 256], tttT[:, 1, j, b, :], WT02[:, b, j, :, :, :],
                                        start=True, stop=True)
                mm_.then_inc(S["gba_ps"].sem, 1)

            def DH(c):
                wait_apart(pe, free(GRAM0, "dh", c, 1, ("A", "dh")), free(GRAM1, "dh", c, 1))
                for b in range(BATCH):
                    for j in range(2):
                        at = ((b % 2) * 2 + j) * P
                        mm_ = pe.matmul(BANK[GRAM0 + b // 2][:, at:at + P], tttT[:, 2, j, b, :], W1D[:, b, j, :, :],
                                        start=True, stop=True)
                mm_.then_inc(S["dh_ps"].sem, 1)

            def FW(c, bp):
                wait_apart(pe, free(UPD0, "gT", c, bp + 1, ("gT",)), free(UPD1, "gT", c, bp + 1))
                for ps, kind in ((BANK[UPD0], 0), (BANK[UPD1], 1)):
                    for y_ in range(2):
                        for j in range(2):
                            b = 2 * bp + y_
                            at = (y_ * 2 + j) * P
                            mm_ = pe.matmul(ps[:, at:at + P], WT02[:, b, j, kind, :, :], tttT[:, 0, j, b, :],
                                            start=True, stop=True)
                mm_.then_inc(S["fw_ps"].sem, 1)

            def OUT(c, bp):
                if bp == 0:
                    wait_apart(pe, free(2, "yg", c, 1), free(3, "yg", c, 1), S["gT"](c, 1))
                else:
                    wait_apart(pe, S["gT"](c, 2))
                for y_ in range(2):
                    for j in range(2):
                        b = 2 * bp + y_
                        at = (y_ * 2 + j) * P
                        mm_ = pe.matmul(BANK[2 + bp][:, at:at + P], gT[:, bp, 2 * y_ + j, :], W1T[:, b, j, :, :],
                                        start=True, stop=True)
                mm_.then_inc(S["out_ps"].sem, 1)

            def DW(c, bp):
                for g, bank, left, right, ready in ((G_W1, GRAM0, vl1, hidden, "el"), (G_W2, GRAM1, dhbm, kl2, "dhbm"),
                                                    (G_W0, 0, dgba, kl0, "dgba")):
                    wait_apart(pe, free(bank, "mom", c, g + 1) if bp == 0 else None, S[ready](c, bp + 1))
                    for y_ in range(2):
                        b = 2 * bp + y_
                        for j in range(2):
                            for i in range(2):
                                hd = 2 * i + j
                                lhs = left[:, b, 2 * j + i, :] if g == G_W1 else left[:, bp, 4 * y_ + hd, :]
                                rhs = right[bp][:, 4 * y_ + hd, :] if g == G_W1 else right[:, b, hd, :]
                                mm_ = pe.matmul(BANK[bank][64 * i:64 * i + 64, (2 * b + j) * HD:(2 * b + j + 1) * HD], lhs, rhs,
                                                start=True, stop=True)
                    if bp == 1:
                        mm_.then_inc(S["dw_ps"].sem, 1)

            def SS(bank, c, g):
                ps = take(bank[0], "ss", c, g + 1)
                pe.wait_ge(*S["mom_ss"](c, g + 1))
                pe.matmul(ps[:, 0:8], ones_blk[:, :], m_ss[:, g, :], start=True, stop=True).then_inc(S["ss_ps"].sem, 1)

            def TX(bank, c, it, g):
                ps = take(bank[0], "XT", c, 3 * it + g + 1, ("X",) if it else ())
                if it == 0:
                    pe.wait_ge(*S["x0"](c, g + 1))
                else:
                    pe.wait_ge(*S["X"](c, 3 * (it - 1) + g + 1))
                for b in range(BATCH):
                    mm_ = pe.transpose(ps[:, b * P:(b + 1) * P], X[:, g, 2 * b:2 * b + 2, :], ident[:, :])
                mm_.then_inc(S["xt_ps"].sem, 1)

            def NA(c, it, g):
                wait_apart(pe, free(GRAM0, "A", c, 3 * it + g + 1, ("mom", "A")), free(GRAM1, "A", c, 3 * it + g + 1),
                           S["XT"](c, 3 * it + g + 1))
                for b in range(BATCH):
                    for i, j in ((0, 0), (1, 1), (0, 1), (1, 0)):
                        half_ = XT[64 * j:64 * j + 64, g, 2 * b + i, :]
                        mm_ = pe.matmul(BANK[GRAM0 + j][64 * i:64 * i + 64, b * HD:(b + 1) * HD], half_, half_,
                                        start=True, stop=True)
                mm_.then_inc(S["a_ps"].sem, 1)

            def NB(bank, c, it, g):
                ps = BANK[bank[0]]
                wait_apart(pe, free(bank[0], "B", c, 3 * it + g + 1), S["A"](c, 3 * it + g + 1))
                for slot in range(8):
                    for i in range(2):
                        a = A[64 * i:64 * i + 64, g, slot, :]
                        mm_ = pe.matmul(ps[64 * i:64 * i + 64, slot * HD:(slot + 1) * HD], a, a, start=True, stop=True)
                mm_.then_inc(S["b_ps"].sem, 1)

            def NX(bank, c, it, g):
                ps = BANK[bank[0]]
                wait_apart(pe, free(bank[0], "X", c, 3 * it + g + 1, ("B",)), S["B"](c, 3 * it + g + 1))
                for slot in range(8):
                    for i in range(2):
                        mm_ = pe.matmul(ps[64 * i:64 * i + 64, slot * HD:(slot + 1) * HD], B[64 * i:64 * i + 64, g, slot, :],
                                        X[64 * i:64 * i + 64, g, slot, :], start=True, stop=True)
                mm_.then_inc(S["x_ps"].sem, 1)

            def WX(bank, c, g):
                ps = take(bank[0], "WT", c, g + 1)
                pe.wait_ge(*S["W"](c, g + 1))
                for b in range(BATCH):
                    mm_ = pe.transpose(ps[:, b * P:(b + 1) * P], W[:, g, 2 * b:2 * b + 2, :], ident[:, :])
                mm_.then_inc(S["w_ps"].sem, 1)

            def SC(bank, c, b):
                ps = take(bank[0], "masked", c, b + 1)
                if b == 0:
                    pe.wait_ge(*S["att_T"](c + 1, 0))
                    pe.wait_ge(*S["k_prev"](c, 0))
                    pe.wait_ge(state_zeroed, 1)
                for hd in range(NAH):
                    mm_ = pe.matmul(ps[:, hd * 256:(hd + 1) * 256], aqT[:, hd, b, :], akT[:, hd, b, :, :], start=True, stop=True)
                mm_.then_inc(S["s_ps"].sem, 1)

            def PT(bank, c, b):
                ps = take(bank[0], "pT", c, b + 1)
                pe.wait_ge(*S["prob"](c, b + 1))
                for n in range(4):
                    mm_ = pe.transpose(ps[:, n * P:(n + 1) * P], prob[:, b % 2, n // 2, (n % 2) * P:(n % 2 + 1) * P], ident[:, :])
                mm_.then_inc(S["pt_ps"].sem, 1)

            def PV(bank, c, b):
                ps = take(bank[0], "comb", c, b + 1, ("pT",))
                if b == 0:
                    pe.wait_ge(*S["v_prev"](c, 0))
                    pe.wait_ge(state_zeroed, 1)
                pe.wait_ge(*S["pT"](c, b + 1))
                for hd in range(NAH):
                    for n in range(2):
                        val = v_prev[:, b, hd * P:(hd + 1) * P] if n == 0 else raw[:, b, 512 + hd * P:512 + (hd + 1) * P]
                        mm_ = pe.matmul(ps[:, hd * P:(hd + 1) * P], pT[:, b % 2, hd, n, :], val, start=(n == 0), stop=(n == 1))
                mm_.then_inc(S["pv_ps"].sem, 1)

            def CT(bank, c, b):
                ps = take(bank[0], "cT", c, b + 1, ("comb",))
                pe.wait_ge(*S["comb"](c, b + 1))
                for k in range(KC):
                    mm_ = pe.transpose(ps[:, k * P:(k + 1) * P], comb[:, b, k * P:(k + 1) * P], ident[:, :])
                mm_.then_inc(S["ct_ps"].sem, 1)

            def WO(bank, c, b):
                pe.wait_ge(ld_wo, 16)
                ps = take(bank[0], "wo_n", c, b + 1, ("cT",))
                pe.wait_ge(*S["cT"](c, b + 1))
                for k in range(KC):
                    mm_ = pe.matmul(ps[:, 0:DIM], cT[:, b % 2, k, :], wo[:, k, :], start=(k == 0), stop=(k == KC - 1))
                mm_.then_inc(S["wo_ps"].sem, 1)

            def NT(bank, c, b):
                ps = take(bank[0], "xn2T", c, b + 1)
                pe.wait_ge(*S["xn2"](c, b + 1))
                for k in range(KC):
                    mm_ = pe.transpose(ps[:, k * P:(k + 1) * P], xn2[:, b, k * P:(k + 1) * P], ident[:, :])
                mm_.then_inc(S["nt_ps"].sem, 1)

            def MT(bank, c, n):
                ps = take(bank[0], "mlp_T", c, n + 1)
                pe.wait_ge(ld_p1 if n < 4 else ld_p2, 16)
                for q in range(4):
                    if n < 4:
                        blk = p1_raw[:, 4 * (n % 2) + q, (n // 2) * P:(n // 2 + 1) * P]
                    else:
                        col = (2 * (n - 4) + q // 2) * P
                        blk = p2_raw[:, q % 2, col:col + P]
                    mm_ = pe.transpose(ps[:, q * P:(q + 1) * P], blk, ident[:, :])
                mm_.then_inc(S["mt_ps"].sem, 1)

            def F1(bank, c, n, part=None):
                at, k_th = (slice(0, 512), n + 1) if part is None else (slice(256 * part, 256 * part + 256), HC * part + n + 1)
                ps = take(bank[0], "h", c, k_th, ("xn2T",) if n == 0 else ())
                if n == 0:
                    pe.wait_ge(*S["xn2T"](c, 2 if part == 0 else 4))
                for k in range(KC):
                    mm_ = pe.matmul(ps[:, at], p1T[:, k, n * P:(n + 1) * P], xn2T[:, k, at], start=(k == 0), stop=(k == KC - 1))
                mm_.then_inc(S["f1_ps"].sem, 1)

            def F2(bank, c, b):
                last_chunk = isinstance(c, int)
                new = b == 0 or (last_chunk and b == 2)
                ps = take(bank[0], "f2", c, b + 1, ("h",) if new else ())
                if new:
                    pe.wait_ge(*S["h"](c, HC if b == 0 else 2 * HC))
                for n in range(HC):
                    mm_ = pe.matmul(ps[:, 0:DIM], h[:, n, b * P:(b + 1) * P], p2T[:, n, :], start=(n == 0), stop=(n == HC - 1))
                mm_.then_inc(S["f2_ps"].sem, 1)

            of_next = {"XT": XT_, "MM": MM, "QK": QK, "VV": VV, "TR": TR, "WX": WX, "MT": MT}
            of_this = {"GB": GB, "DH": DH, "FW": FW, "OUT": OUT, "DW": DW, "SS": SS, "TX": TX, "NA": NA, "NB": NB, "NX": NX,
                       "S": SC, "PT": PT, "PV": PV, "CT": CT, "WO": WO, "NT": NT, "F1": F1, "F2": F2}

            def run(steps, c):
                plan = bank_plan(steps)
                for step in steps:
                    kind, *arg = step
                    bank = [plan[step]] if step in plan else []
                    if kind in of_next:
                        of_next[kind](*bank, c + 1, *arg)
                    elif kind in of_this:
                        of_this[kind](*bank, c, *arg)

            pe.wait_ge(consts, 1)
            run(FIRST, -1)
            pe.wait_ge(*S["mlp_T"](0, 8))
            with pe.Fori(0, CHUNKS - 1) as c:
                all_read_out(c)
                run(BODY, c)
            all_read_out(CHUNKS - 1)
            run(LAST, CHUNKS - 1)

        @block.scalar
        def _(act):
            for name in RAISED_AHEAD["scalar"]:
                act.sem_inc(S[name].sem)
            def copy(dst, src):
                return act.activation(dst, src, ACT.Copy)

            def XT_(bank, c):
                for k in range(KC):
                    act.wait_ge(*S["xT_ps"](c, k + 1))
                    if k == 0:
                        act.wait_ge(*S["v_ps"](c, 0))
                    copy(xnT[:, k, :], BANK[bank[k]]).then_inc(S["xnT"].sem, 1)

            def SP(c):
                act.preload_act_table_set("natural_log_exp_and_others")
                act.wait_ge(*S["lr_neg"](c, 1))
                act.activation(lr_exp[:, :, :], lr_neg[:, :, :], ACT.Exp).then_inc(S["lr_exp"].sem, 1)
                act.wait_ge(*S["lr_exp"](c, 1))
                act.activation(lr_log[:, :, :], lr_exp[:, :, :], ACT.Ln, bias=1.0).then_inc(S["lr_log"].sem, 1)

            def MS(c):
                act.preload_act_table_set("gelu_and_others")
                act.wait_ge(*S["v_raw"](c, 4))
                act.activation(ms_t[:, :, :], small[:, :, 12:20], ACT.Tanh, scale=0.5).then_inc(S["ms_tanh"].sem, 1)

            def QK(bank, c, b):
                act.wait_ge(*S["qk_ps"](c, b + 1))
                act.wait_ge(*S["tr_ps"](c, 0))
                act.wait_ge(*S["silu"](c, 0))
                copy(raw[:, b, 0:512], BANK[bank[0]]).then_inc(S["qk_raw"].sem, 1)

            def SI(c, b):
                act.wait_ge(*S["v_raw"](c, b + 1))
                act.wait_ge(*S["qk_raw"](c, b + 1))
                act.wait_ge(*S["klv"](c, 0))
                act.wait_ge(*S["tr_ps"](c, 0))
                act.activation(silu[:, b, 0:512], raw[:, b, 0:512], ACT.Tanh, scale=0.5)
                act.activation(silu[:, b, 512:768].rearrange("p (j r d) -> p r j d", j=2, r=2),
                               raw[:, b, 512:768].rearrange("p (r j d) -> p r j d", j=2, r=2), ACT.Tanh, scale=0.5)\
                    .then_inc(S["sig"].sem, 1)

            def SQ(c, b):
                act.wait_ge(*S["silu"](c, b + 1))
                if b >= 2:
                    act.wait_ge(*S["ssq"](c, b - 1))
                if b == 0:
                    act.wait_ge(*S["comb"](c, 0))
                act.activation(sq[:, b % 2, :], silu[:, b, 0:512], ACT.Square).then_inc(S["sq"].sem, 1)

            def TR(bank, c, u):
                ps = BANK[bank[0]]
                if u >= 4:
                    return
                kind, hd = divmod(u, 2)
                act.wait_ge(ld_misc, MISC)
                act.wait_ge(*S["tr_ps"](c, u + 1))
                if kind == 0:
                    act.wait_ge(*S["s_ps"](c, 0))
                    dst = aqT[:, hd, :, :]
                else:
                    act.wait_ge(*S["k_prev"](c, 0))
                    dst = akT[:, hd, :, 1, :]
                act.activation(dst, ps.rearrange("p (b t) -> p b t", b=BATCH), ACT.Identity,
                               bias=qk_of[:, hd, kind:kind + 1], scale=qk_sc[:, hd, kind:kind + 1]).then_inc(S["att_T"].sem, 1)

            def GB(c, bp):
                act.wait_ge(*S["gba_ps"](c, bp + 1))
                act.wait_ge(*S["dgba"](c, 0))
                act.wait_ge(*S["one_t"](c, 0))
                gba = work[bp][:, :, :].rearrange("p y (j k e) -> p (y j) k e", j=2, k=2)[:, :, 0, :]
                act.activation(gba_t[:, bp, :, :].rearrange("p (s e) d -> p s (e d)", e=2), gba, ACT.Tanh, scale=0.5).then_inc(S["gba_tanh"].sem, 1)
                act.wait_ge(*S["gba_tanh"](c, bp + 1))
                act.wait_ge(*S["dsig"](c, 0))
                act.activation(one_t[:, bp, :, :], gba_t[:, bp, :, :], ACT.Copy, bias=1.0).then_inc(S["one_t"].sem, 1)

            def DH(c):
                act.wait_ge(*S["dh_ps"](c, 1))
                act.wait_ge(*S["dhbm"](c, 0))
                for bp in range(2):
                    for j in range(2):
                        last = copy(dh[:, bp, :, :, j, :], gram[:, bp, :].rearrange("p (y j r d) -> p y j r d", y=2, j=2, r=2)[:, :, j, :, :])
                last.then_inc(S["dh"].sem, 1)

            def FW(c, bp):
                act.wait_ge(*S["fw_ps"](c, bp + 1))
                act.wait_ge(*S["fw_silu"](c, 0))
                act.activation(fw_t[:, bp, :], upd[0][:, :], ACT.Tanh, scale=0.5).then_inc(S["fw_tanh"].sem, 1)

            def OE(c):
                act.wait_ge(*S["out_ps"](c, 2))
                for bp in range(2):
                    last = act.activation(out_sq[:, bp, :, :], work[1][:, bp, :].rearrange("p (s d) -> p s d", d=HD), ACT.Square)
                last.then_inc(S["out_sq"].sem, 1)

            def MU(c, g):
                act.wait_ge(*S["mom"](c, g + 1))
                act.activation(m_sq[:, g, :, :], M[:, g, :, :], ACT.Square).then_inc(S["mom_sq"].sem, 1)

            def TX(bank, c, it, g):
                act.wait_ge(*S["xt_ps"](c, 3 * it + g + 1))
                copy(XT[:, g, :, :], BANK[bank[0]].rearrange("p (s d) -> p s d", d=HD)).then_inc(S["XT"].sem, 1)

            def NA(c, it, g):
                act.wait_ge(*S["a_ps"](c, 3 * it + g + 1))
                if it:
                    act.wait_ge(*S["B"](c, 3 * (it - 1) + g + 1))
                copy(A[:, g, :, :].rearrange("p (b j) d -> p j b d", j=2),
                     gram[:, :, 0:256].rearrange("p j (b d) -> p j b d", d=HD)).then_inc(S["A"].sem, 1)

            def RN(c, g):
                act.wait_ge(*S["X"](c, 3 * (NIT - 1) + g + 1))
                act.activation(u_sq[:, g, :, :], U[:, g, :, :], ACT.Square).then_inc(S["u_sq"].sem, 1)

            def WX(bank, c, g):
                act.wait_ge(state_zeroed, 1)
                act.wait_ge(*S["w_ps"](c, g + 1))
                ps = BANK[bank[0]].rearrange("p (b j d) -> p b j d", b=BATCH, j=2)
                if g == G_W1:
                    act.wait_ge(*S["out_ps"](c, 0))
                    dst = W1T[:, :, :, :, :]
                else:
                    act.wait_ge(*S["fw_ps"](c, 0))
                    act.wait_ge(*S["gba_ps"](c, 0))
                    dst = WT02[:, :, :, 0 if g == G_W0 else 1, :, :]
                for r in range(2):
                    last = copy(dst[64 * r:64 * r + 64, :, :, r, :], ps[64 * r:64 * r + 64])
                last.then_inc(S["WT"].sem, 1)
                if g == G_W1:
                    act.wait_ge(*S["dh_ps"](c, 0))
                    for r in range(2):
                        last = copy(W1D[64 * r:64 * r + 64, :, :, r, :],
                                    W[64 * r:64 * r + 64, G_W1, :, :].rearrange("p (b j) d -> p b j d", j=2))
                    last.then_inc(S["W1D"].sem, 1)

            def SC(c, b):
                if b == 0:
                    act.preload_act_table_set("natural_log_exp_and_others")
                act.wait_ge(*S["neg_max"](c, b + 1))
                if b >= 2:
                    act.wait_ge(*S["pt_ps"](c, b - 1))
                else:
                    act.wait_ge(*S["pt_ps"](c, 0))
                    act.wait_ge(*S["psum_r"](c, 0))
                for hd in range(NAH):
                    last = act.activation(prob[:, b % 2, hd, :], masked[:, b % 2, hd, :], ACT.Exp, bias=nmax[:, b, hd:hd + 1],
                                          scale=SCALE, accum_out=psums[:, b, hd:hd + 1])
                last.then_inc(S["prob"].sem, 1)

            def PT(bank, c, b):
                act.wait_ge(*S["pt_ps"](c, b + 1))
                if b >= 2:
                    act.wait_ge(*S["pv_ps"](c, b - 1))
                copy(pT[:, b % 2, :, :, :].rearrange("p h n t -> p (h n t)"), BANK[bank[0]]).then_inc(S["pT"].sem, 1)

            def CT(bank, c, b):
                act.wait_ge(*S["ct_ps"](c, b + 1))
                if b >= 2:
                    act.wait_ge(*S["wo_ps"](c, b - 1))
                copy(cT[:, b % 2, :, :].rearrange("p k t -> p (k t)"), BANK[bank[0]][:, 0:256]).then_inc(S["cT"].sem, 1)

            def NT(bank, c, b):
                act.wait_ge(*S["nt_ps"](c, b + 1))
                copy(xn2T[:, :, b * P:(b + 1) * P], BANK[bank[0]][:, 0:256].rearrange("p (k t) -> p k t", k=KC))\
                    .then_inc(S["xn2T"].sem, 1)

            def WI(c):
                act.wait_ge(*S["W"](0, 3))
                for g in range(3):
                    last = act.activation(u_sq[:, g, 0:2, :], W[:, g, 0:2, :], ACT.Square)
                last.then_inc(S["w_sq"].sem, 1)

            def MT(bank, c, n):
                act.wait_ge(*S["mt_ps"](c, n + 1))
                if n < 4:
                    last = copy(p1T[:, n // 2, (n % 2) * 512:(n % 2 + 1) * 512], BANK[bank[0]])
                else:
                    last = copy(p2T[:, 2 * (n - 4):2 * (n - 4) + 2, :].rearrange("p a b -> p (a b)"), BANK[bank[0]])
                last.then_inc(S["mlp_T"].sem, 1)

            def F1(bank, c, n, part=None):
                at, k_th = (slice(0, 512), n + 1) if part is None else (slice(256 * part, 256 * part + 256), HC * part + n + 1)
                act.wait_ge(*S["f1_ps"](c, k_th))
                if n == 0:
                    act.wait_ge(*S["f2_ps"](c, 0))
                act.activation(h[:, n, at], BANK[bank[0]][:, at], ACT.Gelu, bias=b1[:, n:n + 1]).then_inc(S["h"].sem, 1)

            of_next = {"XT": XT_, "SP": SP, "MS": MS, "QK": QK, "SI": SI, "NQ": SQ, "TR": TR, "WX": WX, "WI": WI, "MT": MT}
            of_this = {"GB": GB, "DH": DH, "FW": FW, "OE": OE, "MU": MU, "TX": TX, "NA": NA, "RN": RN, "S": SC, "PT": PT,
                       "CT": CT, "NT": NT, "F1": F1}
            READS = ("XT", "QK", "TR", "WX", "MT", "TX", "PT", "CT", "NT", "F1")

            def run(steps, c):
                plan = bank_plan(steps)
                for step in steps:
                    kind, *arg = step
                    bank = [plan[step]] if kind in READS else []
                    if kind in of_next:
                        of_next[kind](*bank, c + 1, *arg)
                    elif kind in of_this:
                        of_this[kind](*bank, c, *arg)

            act.preload_act_table_set("gelu_and_others")
            act.wait_ge(consts, 1)
            run(FIRST, -1)
            act.wait_ge(*S["w_ss"](0, 1))
            with act.Fori(0, CHUNKS - 1) as c:
                run(BODY, c)
            run(LAST, CHUNKS - 1)

        @block.vector
        def _(dve):
            for name in RAISED_AHEAD["vector"]:
                dve.sem_inc(S[name].sem)
            def stt(out_, in0, scalar, in1, op0, op1):
                return dve.scalar_tensor_tensor(out=out_, in0=in0, scalar=scalar, in1=in1, op0=op0, op1=op1)

            def LN1(c):
                dve.wait_ge(*S["x_in"](c, 16))
                dve.wait_ge(*S["xT_ps"](c, 0))
                for b in range(BATCH):
                    last = dve.bn_stats(st1[:, b, :], x_in[:, b, :])
                last.then_inc(S["ln1_stats"].sem, 1)
                wait_apart(dve, S["ln1_stats"](c, 1))
                for b in range(BATCH):
                    last = dve.bn_aggr(mv1[:, b, :], st1[:, b, :])
                last.then_inc(S["ln1_mv"].sem, 1)

            def LNX(c):
                dve.wait_ge(*S["ln1_rstd"](c, 1))
                for b in range(BATCH):
                    last = dve.tensor_scalar(xn[:, b, :], x_in[:, b, :], mv1[:, b, 0:1], rstd1[:, b:b + 1],
                                             ALU.subtract, ALU.mult)
                last.then_inc(S["xn"].sem, 1)

            def SM(c):
                dve.wait_ge(*S["v_raw"](c, 4))
                dve.wait_ge(*S["lr_log"](c, 0))
                z = small[:, :, 0:12]
                stt(lr_neg[:, :, :], z, -1.0, z, ALU.mult, ALU.min).then_inc(S["lr_neg"].sem, 1)

            def SP(c):
                dve.wait_ge(*S["lr_log"](c, 1))
                dve.wait_ge(*S["klv"](c, 0))
                stt(lr[:, :, :], small[:, :, 0:12], 0.0, lr_log[:, :, :], ALU.max, ALU.add).then_inc(S["lr"].sem, 1)

            def MS(c):
                dve.wait_ge(*S["ms_tanh"](c, 1))
                dve.wait_ge(*S["out_f"](c, 0))
                dve.wait_ge(*S["mm_ps"](c, 0))
                dve.tensor_scalar(ms[:, :, 0:4], ms_t[:, :, 0:4], 1.0, None, ALU.add)
                stt(ms[:, :, 4:8], ms_t[:, :, 4:8], 1.0, small[:, :, 16:20], ALU.add, ALU.mult).then_inc(S["ms"].sem, 1)

            def MM(bank, c):
                dve.wait_ge(*S["mm_ps"](c, 1))
                dve.wait_ge(*S["decayed"](c, 0))
                dve.tensor_copy(mm[:, :], BANK[bank[0]][:, 0:8]).then_inc(S["mm"].sem, 1)

            def VV(bank, c, b):
                dve.wait_ge(*S["v_ps"](c, b + 1))
                dve.wait_ge(*S["v_prev"](c, 0))
                dve.tensor_copy(raw[:, b, 512:768], BANK[bank[0]][:, 0:DIM])
                if b == 0:
                    dve.wait_ge(ld_misc, MISC)
                    dve.wait_ge(*S["ms"](c, 0))
                    dve.wait_ge(*S["lr"](c, 0))
                dve.tensor_tensor(small[:, b, :], BANK[bank[0]][:, DIM:DIM + SMALL], small_bias[:, :], ALU.add)\
                    .then_inc(S["v_raw"].sem, 1)

            def SI(c, b):
                dve.wait_ge(*S["sig"](c, b + 1))
                dve.wait_ge(*S["klv"](c, 0))
                dve.wait_ge(*S["tr_ps"](c, 0))
                stt(silu[:, b, 0:512], silu[:, b, 0:512], 1.0, raw[:, b, 0:512], ALU.add, ALU.mult)
                th = silu[:, b, 512:768].rearrange("p (j r d) -> p j r d", j=2, r=2)
                val = raw[:, b, 512:768].rearrange("p (r j d) -> p j r d", j=2, r=2)
                for j in range(2):
                    last = stt(th[:, j, :, :], th[:, j, :, :], 1.0, val[:, j, :, :], ALU.add, ALU.mult)
                last.then_inc(S["silu"].sem, 1)

            def NQ(c, b):
                dve.wait_ge(*S["sq"](c, b + 1))
                dve.tensor_reduce(ssq[:, b, :], sq[:, b % 2, :].rearrange("p (h d) -> p h d", d=HD), AX.X, ALU.add)\
                    .then_inc(S["ssq"].sem, 1)

            def NR(c, b):
                dve.wait_ge(*S["nq"](c, b + 1))
                dve.tensor_scalar(nqe[:, b, :], nq[:, b, :], 2.0e-5, None, ALU.add).then_inc(S["nq_eps"].sem, 1)
                dve.wait_ge(*S["nq_eps"](c, b + 1))
                dve.reciprocal(rq[:, b, :], nqe[:, b, :]).then_inc(S["rq"].sem, 1)

            def TR(bank, c, u):
                ps = BANK[bank[0]]
                if u < 4:
                    return
                kind, j = divmod(u - 4, 2)
                dve.wait_ge(*S["tr_ps"](c, u + 1))
                if u == 4:
                    dve.wait_ge(*S["fw_ps"](c, 0))
                    dve.wait_ge(*S["gba_ps"](c, 0))
                    dve.wait_ge(*S["dh_ps"](c, 0))
                dve.tensor_copy(tttT[:, kind, j, :, :].rearrange("p b t -> p (b t)"), ps).then_inc(S["ttt_T"].sem, 1)

            def EL(c, bp):
                both = work[bp][:, :, :].rearrange("p y (j k e) -> p (y j) k e", j=2, k=2)
                gba, hbm = both[:, :, 0, :], both[:, :, 1, :]

                def pairs(t):
                    return t.rearrange("p (s e) d -> p s (e d)", e=2)

                dhs = dh[:, bp, :, :, :, :].rearrange("p y r j d -> p (y r) (j d)")
                dve.wait_ge(*S["gba_tanh"](c, bp + 1))
                if bp == 0:
                    dve.wait_ge(*S["dhbm"](c, 0))
                    dve.wait_ge(*S["dw_ps"](c, 0))
                stt(pairs(sg[:, bp, :, :]), pairs(gba_t[:, bp, :, :]), 1.0, gba, ALU.add, ALU.mult).then_inc(S["sg"].sem, 1)
                dve.wait_ge(*S["dh"](c, 1))
                dve.tensor_tensor(pairs(dxh[:, bp, :, :]), dhs, hbm, ALU.mult)
                dve.wait_ge(*S["sg"](c, bp + 1))
                dve.tensor_tensor(pairs(hidden[bp]), pairs(sg[:, bp, :, :]), hbm, ALU.mult)
                stt(pairs(gms[:, bp, :, :]), pairs(sg[:, bp, :, :]), -0.5, gba, ALU.mult, ALU.add).then_inc(S["el"].sem, 1)

            def ELB(c, bp):
                dve.wait_ge(*S["one_t"](c, bp + 1))
                dve.wait_ge(*S["el"](c, bp + 1))
                stt(dsig[:, bp, :, :], gms[:, bp, :, :], 1.0, one_t[:, bp, :, :], ALU.add, ALU.mult).then_inc(S["dsig"].sem, 1)
                dve.wait_ge(*S["dsig"](c, bp + 1))
                dve.tensor_tensor(dgba[:, bp, :, :], dxh[:, bp, :, :], dsig[:, bp, :, :], ALU.mult).then_inc(S["dgba"].sem, 1)

            def FE(c, bp):
                dve.wait_ge(*S["fw_tanh"](c, bp + 1))
                stt(fw_s[:, bp, :], fw_t[:, bp, :], 1.0, upd[0][:, :], ALU.add, ALU.mult).then_inc(S["fw_silu"].sem, 1)
                dve.wait_ge(*S["fw_silu"](c, bp + 1))
                dve.wait_ge(*S["out_ps"](c, 0))
                dve.tensor_tensor(gT[:, bp, :, :].rearrange("p s t -> p (s t)"), fw_s[:, bp, :], upd[1][:, :], ALU.mult)\
                    .then_inc(S["gT"].sem, 1)

            def OE(c):
                dve.wait_ge(*S["out_sq"](c, 1))
                dve.tensor_reduce(out_ms[:, :, :].rearrange("p b h -> p (b h)"),
                                  out_sq[:, :, :, :].rearrange("p r s d -> p (r s) d"), AX.X, ALU.add)\
                    .then_inc(S["out_ms"].sem, 1)
                dve.wait_ge(*S["comb"](c, 0))
                dve.wait_ge(*S["ssq"](c, 4))
                for bp in range(2):
                    last = dve.tensor_tensor(y[:, 2 * bp:2 * bp + 2, :, :].rearrange("p y h d -> p (y h) d"),
                                             work[1][:, bp, :].rearrange("p (s d) -> p s d", d=HD),
                                             g_half[:, :].unsqueeze(1).to_broadcast([P, 8, HD]), ALU.mult)
                last.then_inc(S["yg"].sem, 1)

            def OY(c):
                dve.wait_ge(*S["yg"](c, 1))
                dve.wait_ge(*S["out_f"](c, 1))
                dve.tensor_tensor(y[:, :, :, :].rearrange("p b h d -> p (b h) d"), y[:, :, :, :].rearrange("p b h d -> p (b h) d"),
                                  bcast(out_f[:, :, :].rearrange("p b h -> p (b h)"), HD), ALU.mult).then_inc(S["y"].sem, 1)

            def MU(c, g):
                bank = (GRAM0, GRAM1, 0)[g]
                dve.wait_ge(*S["dw_ps"](c, g + 1))
                dve.wait_ge(*S["decayed"](c + 1, 0))
                dve.tensor_tensor(M[:, g, :, :], BANK[bank].rearrange("p (s d) -> p s d", d=HD), decayed[:, g, :, :], ALU.add)\
                    .then_inc(S["mom"].sem, 1)

            def SS(bank, c, g):
                ps = BANK[bank[0]]
                dve.wait_ge(*S["ss_ps"](c, g + 1))
                dve.tensor_copy(ss[:, g, :], ps[:, 0:8]).then_inc(S["ss"].sem, 1)

            def MR(c, g):
                dve.wait_ge(*S["mom_sq"](c, g + 1))
                dve.tensor_reduce(m_ss[:, g, :], m_sq[:, g, :, :], AX.X, ALU.add).then_inc(S["mom_ss"].sem, 1)

            def SN(c, g):
                dve.wait_ge(*S["fro"](c, g + 1))
                dve.tensor_scalar(fro_e[:, g, :], fro[:, g, :], GRAD_GAIN * 1e-7, None, ALU.add).then_inc(S["fro_eps"].sem, 1)
                dve.wait_ge(*S["fro_eps"](c, g + 1))
                dve.reciprocal(rfro[:, g, :], fro_e[:, g, :]).then_inc(S["rfro"].sem, 1)
                dve.wait_ge(*S["rfro"](c, g + 1))
                dve.wait_ge(*S["x_ps"](c, 0))
                dve.tensor_tensor(X[:, g, :, :], M[:, g, :, :], bcast(rfro[:, g, :], HD), ALU.mult).then_inc(S["x0"].sem, 1)

            def NB(bank, c, it, g):
                ps = BANK[bank[0]].rearrange("p (s d) -> p s d", d=HD)
                dve.wait_ge(*S["b_ps"](c, 3 * it + g + 1))
                if it:
                    dve.wait_ge(*S["x_ps"](c, 3 * (it - 1) + g + 1))
                stt(B[:, g, :, :], ps, NS_F[it], A[:, g, :, :], ALU.mult, ALU.add).then_inc(S["B"].sem, 1)

            def NX(bank, c, it, g):
                ps = BANK[bank[0]].rearrange("p (s d) -> p s d", d=HD)
                dve.wait_ge(*S["x_ps"](c, 3 * it + g + 1))
                if it < NIT - 1:
                    stt(X[:, g, :, :], ps, NS_E[it], X[:, g, :, :], ALU.mult, ALU.add).then_inc(S["X"].sem, 1)
                else:
                    dve.wait_ge(*S["V"](c, g + 1))
                    stt(U[:, g, :, :], ps, NS_E[it] * NS_S, V[:, g, :, :], ALU.mult, ALU.add).then_inc(S["X"].sem, 1)

            def NV(c, g):
                dve.wait_ge(*S["X"](c, 3 * (NIT - 2) + g + 1))
                stt(V[:, g, :, :], X[:, g, :, :], NS_S, W[:, g, :, :], ALU.mult, ALU.add).then_inc(S["V"].sem, 1)

            def RN(c, g):
                dve.wait_ge(*S["u_sq"](c, g + 1))
                dve.tensor_reduce(u_ss[:, g, :], u_sq[:, g, :, :], AX.X, ALU.add).then_inc(S["u_ss"].sem, 1)

            def RM(c, g):
                dve.wait_ge(*S["u_n"](c, g + 1))
                dve.tensor_scalar(u_e[:, g, :], u_n[:, g, :], 1e-5, None, ALU.add).then_inc(S["u_eps"].sem, 1)
                dve.wait_ge(*S["u_eps"](c, g + 1))
                dve.reciprocal(u_r[:, g, :], u_e[:, g, :]).then_inc(S["u_r"].sem, 1)
                dve.wait_ge(*S["u_r"](c, g + 1))
                dve.tensor_tensor(u_f[:, g, :].rearrange("p (b j) -> p b j", j=2), u_r[:, g, :].rearrange("p (b j) -> p b j", j=2),
                                  row_norm[:, g, :].unsqueeze(1).to_broadcast([P, BATCH, 2]), ALU.mult).then_inc(S["u_f"].sem, 1)
                dve.wait_ge(*S["u_f"](c, g + 1))
                dve.tensor_tensor(W[:, g, :, :], U[:, g, :, :], bcast(u_f[:, g, :], HD), ALU.mult).then_inc(S["W"].sem, 1)

            def SC(bank, c, b):
                ps = BANK[bank[0]]
                wait_apart(dve, S["s_ps"](c, b + 1), S["pt_ps"](c, max(b - 1, 0)), S["m_prev"](c, 0))
                for hd in range(NAH):
                    last = dve.tensor_tensor_reduce(masked[:, b % 2, hd, :], ps[:, hd * 256:(hd + 1) * 256], mask[:, :], 1.0,
                                                    -3.0e38, ALU.add, ALU.max, smax[:, b, hd:hd + 1])
                last.then_inc(S["masked"].sem, 1)
                dve.wait_ge(*S["masked"](c, b + 1))
                dve.tensor_scalar(nmax[:, b, :], smax[:, b, :], -SCALE, None, ALU.mult).then_inc(S["neg_max"].sem, 1)

            def PT(c, b):
                dve.wait_ge(*S["prob"](c, b + 1))
                dve.wait_ge(*S["comb"](c, 0))
                dve.reciprocal(rsums[:, b, :], psums[:, b, :]).then_inc(S["psum_r"].sem, 1)

            def PV(bank, c, b):
                ps = BANK[bank[0]]
                dve.wait_ge(*S["pv_ps"](c, b + 1))
                dve.wait_ge(*S["y"](c, 1))
                dve.wait_ge(*S["psum_r"](c, b + 1))
                dve.wait_ge(*S["ct_ps"](c, 0))
                for hd in range(NAH):
                    last = stt(comb[:, b, hd * P:(hd + 1) * P], ps[:, hd * P:(hd + 1) * P], rsums[:, b, hd:hd + 1],
                               y[:, b, 2 * hd:2 * hd + 2, :].rearrange("p h d -> p (h d)"), ALU.mult, ALU.add)
                last.then_inc(S["comb"].sem, 1)

            wo_ps = {}

            def WO(bank, c, b):
                wo_ps[b] = ps = BANK[bank[0]]
                dve.wait_ge(*S["wo_ps"](c, b + 1))
                dve.bn_stats(st2[:, b, :], ps[:, 0:DIM]).then_inc(S["wo_st"].sem, 1)
                wait_apart(dve, S["wo_st"](c, b + 1))
                dve.bn_aggr(mv2[:, b, :], st2[:, b, :]).then_inc(S["wo_mv"].sem, 1)

            def WON(c, b):
                dve.wait_ge(*S["wo_rstd"](c, b + 1))
                if b == 0:
                    dve.wait_ge(*S["stored"](c, 0))
                dve.tensor_scalar(wo_n[:, b, :], wo_ps[b][:, 0:DIM], mv2[:, b, 0:1], rstd2[:, b:b + 1], ALU.subtract, ALU.mult)\
                    .then_inc(S["wo_n"].sem, 1)

            def L2(c, b):
                dve.wait_ge(*S["x1"](c, b + 1))
                dve.bn_stats(st3[:, b, :], x1[:, b, :]).then_inc(S["l2_st"].sem, 1)
                wait_apart(dve, S["l2_st"](c, b + 1))
                dve.bn_aggr(mv3[:, b, :], st3[:, b, :]).then_inc(S["l2_mv"].sem, 1)

            def L2N(c, b):
                dve.wait_ge(*S["l2_rstd"](c, b + 1))
                dve.wait_ge(*S["nt_ps"](c, 0))
                dve.tensor_scalar(xn2[:, b, :], x1[:, b, :], mv3[:, b, 0:1], rstd3[:, b:b + 1], ALU.subtract, ALU.mult)\
                    .then_inc(S["xn2"].sem, 1)

            def WI(c):
                dve.wait_ge(ld_w, 96)
                for g in range(3):
                    dve.tensor_copy(W[:, g, :, :].rearrange("p (b j) d -> p b (j d)", j=2),
                                    w_in[:, g, :, :].rearrange("p j d -> p (j d)").unsqueeze(1).to_broadcast([P, BATCH, 2 * HD]))\
                        .then_inc(S["W"].sem, 1)

            def ZS(c):
                for t in (WT02, W1T, W1D):
                    names = "abcde"[:len(t.shape) - 1]
                    dve.memset(t[tuple([slice(None)] * len(t.shape))].rearrange(f"p {' '.join(names)} -> p ({' '.join(names)})"), 0.0)
                dve.memset(v_prev[:, :, :], 0.0)
                dve.memset(akT[:, :, :, 0, :], 0.0)
                dve.memset(M[:, :, :, :], 0.0).then_inc(state_zeroed, 1)

            def WN(c):
                dve.wait_ge(*S["w_sq"](c, 1))
                dve.tensor_reduce(row_ss[:, :, :], u_sq[:, :, 0:2, :], AX.X, ALU.add).then_inc(S["w_ss"].sem, 1)

            def F2(bank, c, b):
                ps = BANK[bank[0]]
                dve.wait_ge(*S["f2_ps"](c, b + 1))
                dve.tensor_tensor(f2[:, b, :], ps[:, 0:DIM], b2[:, :], ALU.add).then_inc(S["f2"].sem, 1)
                dve.wait_ge(*S["f2"](c, b + 1))
                dve.bn_stats(st4[:, b, :], f2[:, b, :]).then_inc(S["f2_st"].sem, 1)
                wait_apart(dve, S["f2_st"](c, b + 1))
                dve.bn_aggr(mv4[:, b, :], st4[:, b, :]).then_inc(S["f2_mv"].sem, 1)

            def F2N(c, b):
                dve.wait_ge(*S["f2_rstd"](c, b + 1))
                dve.wait_ge(*S["outb"](c, 0))
                dve.tensor_scalar(f2_n[:, b, :], f2[:, b, :], mv4[:, b, 0:1], rstd4[:, b:b + 1], ALU.subtract, ALU.mult)\
                    .then_inc(S["f2_n"].sem, 1)

            of_next = {"LN1": LN1, "SM": SM, "SP": SP, "MS": MS, "MM": MM, "VV": VV, "SI": SI, "NQ": NQ, "NR": NR, "TR": TR, "LNX": LNX, "WI": WI, "WN": WN, "ZS": ZS}
            of_this = {"EL": EL, "ELB": ELB, "FE": FE, "OE": OE, "OY": OY, "MU": MU, "MR": MR, "RM": RM, "SS": SS, "SN": SN, "NB": NB, "NX": NX,
                       "NV": NV, "RN": RN, "S": SC, "PT": PT, "PV": PV, "WO": WO, "WON": WON, "L2": L2, "L2N": L2N, "F2": F2,
                       "F2N": F2N}
            READS = ("MM", "VV", "TR", "SS", "NB", "NX", "S", "PV", "WO", "F2")

            def run(steps, c):
                plan = bank_plan(steps)
                for step in steps:
                    kind, *arg = step
                    bank = [plan[step]] if kind in READS else []
                    if kind in of_next:
                        of_next[kind](*bank, c + 1, *arg)
                    elif kind in of_this:
                        of_this[kind](*bank, c, *arg)

            dve.wait_ge(consts, 1)
            run(FIRST, -1)
            dve.tensor_scalar(g_half[:, :], g_raw[:, :], 0.5, None, ALU.mult).then_inc(folded, 1)
            dve.wait_ge(*S["w_norm"](0, 1))
            dve.wait_ge(folded, 1)
            with dve.Fori(0, CHUNKS - 1) as c:
                run(BODY, c)
            run(LAST, CHUNKS - 1)

        @block.gpsimd
        def _(pool):
            for name in RAISED_AHEAD["gpsimd"]:
                pool.sem_inc(S[name].sem)
            def tt(out_, in0, in1, op=ALU.mult):
                return pool.tensor_tensor(out_, in0, in1, op)

            def rsqrt(c, n, mv, var, rstd, ready, mid, done, sl):
                wait_apart(pool, S[ready](c, n))
                pool.tensor_scalar(var[:, sl], mv[:, sl, 1], LN_EPS, None, ALU.add).then_inc(S[mid].sem, 1)
                pool.wait_ge(*S[mid](c, n))
                k = sl.stop - sl.start
                tt(rstd[:, sl], var[:, sl], neg_half[:, 0:k], ALU.pow).then_inc(S[done].sem, 1)

            def LN1(c):
                rsqrt(c, 1, mv1, var1, rstd1, "ln1_mv", "ln1_var", "ln1_rstd", slice(0, BATCH))

            def MP(c):
                pool.wait_ge(state_zeroed, 1)
                pool.wait_ge(*S["mm"](c, 1))
                pool.wait_ge(*S["mom"](c, 0))
                pool.wait_ge(*S["X"](c, 0))
                for g in range(3):
                    tt(decayed[:, g, :, :], M[:, g, :, :], bcast(mm[:, :], HD)).then_inc(S["decayed"].sem, 1)

            def NQ(c, b):
                pool.wait_ge(*S["ssq"](c, b + 1))
                tt(nq[:, b, :], ssq[:, b, :], half[:, 0:8], ALU.pow).then_inc(S["nq"].sem, 1)

            def NR(c, b):
                pool.wait_ge(*S["rq"](c, b + 1))
                tt(qn[:, b, 0:512].rearrange("p (h d) -> p h d", d=HD), silu[:, b, 0:512].rearrange("p (h d) -> p h d", d=HD),
                   bcast(rq[:, b, :], HD)).then_inc(S["qn"].sem, 1)

            def KL(c, b):
                pool.wait_ge(*S["qn"](c, b + 1))
                pool.wait_ge(*S["lr"](c, 1))
                pool.wait_ge(*S["dw_ps"](c, 0))
                rates = lr[:, b, :].rearrange("p (h i) -> p h i", i=3)
                kk = qn[:, b, 256:512].rearrange("p (h d) -> p h d", d=HD)
                tt(kl0[:, b, :, :], kk, bcast(rates[:, :, 0], HD))
                tt(kl2[:, b, :, :], kk, bcast(rates[:, :, 2], HD))
                tt(vl1[:, b, :, :].rearrange("p (j r) d -> p j r d", j=2),
                   silu[:, b, 512:768].rearrange("p (j r d) -> p j r d", j=2, r=2),
                   bcast(rates[:, :, 1].rearrange("p (r j) -> p j r", j=2), HD))\
                    .then_inc(S["klv"].sem, 1)

            def EL(c, bp):
                pool.wait_ge(*S["sg"](c, bp + 1))
                pool.wait_ge(*S["dh"](c, 1))
                tt(dhbm[:, bp, :, :], dh[:, bp, :, :, :, :].rearrange("p y r j d -> p (y r j) d"), sg[:, bp, :, :])\
                    .then_inc(S["dhbm"].sem, 1)

            def OE(c):
                wait_apart(pool, S["out_ms"](c, 1))
                pool.tensor_scalar(out_v[:, :, :], out_ms[:, :, :], 1.0 / HD, 4 * 1e-5, ALU.mult, ALU.add)\
                    .then_inc(S["out_var"].sem, 1)
                pool.wait_ge(*S["out_var"](c, 1))
                tt(out_rs[:, :, :].rearrange("p b h -> p (b h)"), out_v[:, :, :].rearrange("p b h -> p (b h)"),
                   neg_half[:, 0:16], ALU.pow).then_inc(S["out_rs"].sem, 1)
                pool.wait_ge(*S["out_rs"](c, 1))
                tt(out_f[:, :, :], out_rs[:, :, :], ms[:, :, 4:8]).then_inc(S["out_f"].sem, 1)

            def SS(c, g):
                pool.wait_ge(*S["ss"](c, g + 1))
                tt(fro[:, g, :], ss[:, g, :], half[:, 0:8], ALU.pow).then_inc(S["fro"].sem, 1)

            def RN(c, g):
                pool.wait_ge(*S["u_ss"](c, g + 1))
                tt(u_n[:, g, :], u_ss[:, g, :], half[:, 0:8], ALU.pow).then_inc(S["u_n"].sem, 1)

            def PRV(c):
                wait_apart(pool, S["s_ps"](c, 4))
                pool.tensor_copy(akT[:, :, :, 0, :].rearrange("p h b t -> p (h b) t"),
                                 akT[:, :, :, 1, :].rearrange("p h b t -> p (h b) t")).then_inc(S["k_prev"].sem, 1)
                wait_apart(pool, S["pv_ps"](c, 4))
                pool.tensor_copy(v_prev[:, :, :], raw[:, :, 512:768]).then_inc(S["v_prev"].sem, 1)
                wait_apart(pool, S["masked"](c, 4))
                pool.tensor_copy(mask[:, 0:P], mask_prev[:, :]).then_inc(S["m_prev"].sem, 1)

            def WO(c, b):
                rsqrt(c, b + 1, mv2, var2, rstd2, "wo_mv", "wo_var", "wo_rstd", slice(b, b + 1))

            def WON(c, b):
                pool.wait_ge(*S["wo_n"](c, b + 1))
                if b == 0:
                    pool.wait_ge(*S["x_again"](c, 16))
                tt(x1[:, b, :], wo_n[:, b, :], x1[:, b, :], ALU.add).then_inc(S["x1"].sem, 1)

            def L2(c, b):
                rsqrt(c, b + 1, mv3, var3, rstd3, "l2_mv", "l2_var", "l2_rstd", slice(b, b + 1))

            def WN(c):
                pool.wait_ge(*S["w_ss"](c, 1))
                tt(row_norm[:, :, :].rearrange("p g j -> p (g j)"), row_ss[:, :, :].rearrange("p g j -> p (g j)"), half[:, 0:6],
                   ALU.pow).then_inc(S["w_norm"].sem, 1)

            def F2(c, b):
                rsqrt(c, b + 1, mv4, var4, rstd4, "f2_mv", "f2_var", "f2_rstd", slice(b, b + 1))

            def F2N(c, b):
                pool.wait_ge(*S["f2_n"](c, b + 1))
                tt(outb[:, b, :], f2_n[:, b, :], x1[:, b, :], ALU.add).then_inc(S["outb"].sem, 1)

            of_next = {"LN1": LN1, "MP": MP, "NQ": NQ, "NR": NR, "KL": KL, "WN": WN}
            of_this = {"EL": EL, "OE": OE, "SS": SS, "RN": RN, "PRV": PRV, "WO": WO, "WON": WON, 
                       "L2": L2, "F2": F2, "F2N": F2N}

            def run(steps, c):
                for kind, *arg in steps:
                    if kind in of_next:
                        of_next[kind](c + 1, *arg)
                    elif kind in of_this:
                        of_this[kind](c, *arg)

            pool.memset(small_bias[:, 0:12], BASE_LR_INV)
            for t, v in ((ident, 0.0), (ones_blk, 0.0), (ones_avg, 0.5 / CHUNK), (half, 0.5), (neg_half, -0.5),
                         (mask_prev, 0.0), (mask, 0.0)):
                last = pool.memset(t[:, :], v)
            last.then_inc(zeroed, 1)
            pool.wait_ge(zeroed, 1)
            pool.affine_select(out=ident[:, :], in_=ident[:, :], compare_op=ALU.not_equal, fill=1.0, base=0,
                               pattern=[[-1, P]], channel_multiplier=1)
            pool.affine_select(out=mask_prev[:, :], in_=mask_prev[:, :], compare_op=ALU.is_ge, fill=NEG, base=0,
                               pattern=[[1, P]], channel_multiplier=-1)
            pool.affine_select(out=mask[:, P:2 * P], in_=mask[:, P:2 * P], compare_op=ALU.is_ge, fill=NEG, base=0,
                               pattern=[[-1, P]], channel_multiplier=1)
            pool.memset(mask[:, 0:P], NEG)
            pool.memset(ones_blk[0:64, 0:64], 1.0).then_inc(zeroed, 1)
            pool.wait_ge(zeroed, 2)
            pool.memset(ones_blk[64:128, 64:128], 1.0).then_inc(consts, 1)
            pool.wait_ge(consts, 1)
            run(FIRST, -1)
            with pool.Fori(0, CHUNKS - 1) as c:
                run(BODY, c)
            run(LAST, CHUNKS - 1)


_INS = ['L0_attn_x', 'L0_attn_Wqkv', 'L0_attn_Wlr', 'L0_attn_Wm', 'L0_attn_bm', 'L0_attn_Ws', 'L0_attn_bs', 'L0_attn_Wo',
        'L0_attn_w0', 'L0_attn_w1', 'L0_attn_w2', 'L0_attn_o_norm_g', 'L0_attn_qk_scale', 'L0_attn_qk_offset',
        'L0_ffn_proj1', 'L0_ffn_proj1_bias', 'L0_ffn_proj2', 'L0_ffn_proj2_bias']


def kernel(**inputs):
    import concourse.bacc as _bacc
    from concourse.bass_utils import run_bass_kernel_spmd as _run

    nc = _bacc.Bacc("TRN2", target_bir_lowering=False, num_devices=1)
    arrays, args = {}, []
    for name in _INS:
        a = np.ascontiguousarray(inputs[name])
        arrays[f"in_{name}_dram"] = a
        args.append(nc.dram_tensor(f"in_{name}_dram", a.shape, mybir.dt.from_np(a.dtype), kind="ExternalInput").ap())
    args.append(nc.dram_tensor("out_0_dram", (BATCH, SEQ, DIM), F32, kind="ExternalOutput").ap())
    layer_kernel(nc, *args)
    r = _run(nc, [arrays], core_ids=[0])
    return r.results[0]["out_0_dram"]
```
